# Optimizing a Trainium2 kernel written in Bass

```python
import numpy as np
import jax
import jax.numpy as jnp

def _softmax(x, axis=-1):
    return jax.nn.softmax(x, axis=axis)

def _gelu(x):
    return jax.nn.gelu(x, approximate=True)

def _silu(x):
    return jax.nn.silu(x)

def _sigmoid(x):
    return jax.nn.sigmoid(x)

def _layernorm(x, axis=-1, eps=1e-05):
    m = jnp.mean(x, axis=axis, keepdims=True)
    v = jnp.var(x, axis=axis, keepdims=True)
    return (x - m) / jnp.sqrt(v + eps)

def _scatter_add(tgt, idx, src, axis=0):
    return tgt.at[idx].add(src)

def _segment_sum(src, seg, n):
    return jax.ops.segment_sum(src, seg, n)
kernel_name = 'mk_seq_preln_d1_jaxref_r8_1a4e0c'

def setup_inputs(seed: int=0):
    np.random.seed(seed)
    _w = jnp.asarray

    def _L0_attn_setup():
        import jax, jax.numpy as jnp
        import numpy as np
        B, N, D_IN, D_OUT = (4, 256, 128, 128)
        key = jax.random.key(seed)
        k = jax.random.split(key, 6)
        x = jax.random.normal(k[0], (B, N, D_IN), dtype=jnp.float32)
        sc_in = 1.0 / np.sqrt(D_IN)
        sc_out = 1.0 / np.sqrt(D_OUT)
        W_spin = jax.random.uniform(k[1], (D_OUT, D_IN), jnp.float32, -sc_in, sc_in)
        b_spin = jax.random.uniform(k[2], (D_OUT,), jnp.float32, -sc_in, sc_in)
        W_global = jax.random.uniform(k[3], (D_OUT, D_OUT), jnp.float32, -sc_out, sc_out)
        W_J = jax.random.uniform(k[4], (D_OUT, D_OUT), jnp.float32, -sc_out, sc_out)
        beta = jnp.ones((1,), dtype=jnp.float32)
        return {'x': x, 'W_spin': W_spin, 'b_spin': b_spin, 'W_global': W_global, 'W_J': W_J, 'beta': beta}
    _L0_attn_in = _L0_attn_setup()

    def _L0_ffn_setup():
        import jax, jax.numpy as jnp
        import numpy as np
        B, T, C = (2, 256, 128)
        H, D = (16, 64)
        CR = 8
        R = C // CR
        ROPE = D // 2
        NOPE = D - ROPE
        E, K, I, S = (8, 2, 64, 1)
        THETA = 100000.0
        EPS = 1e-05

        def _rmsnorm(x, w):
            rms = jnp.sqrt(jnp.mean(x * x, axis=-1, keepdims=True) + EPS)
            return w * (x / rms)

        def _rope(xh):
            d = xh.shape[-1]
            t = jnp.arange(xh.shape[2], dtype=jnp.float32)
            freqs = 1.0 / THETA ** (jnp.arange(0, d, 2, dtype=jnp.float32) / d)
            ang = jnp.outer(t, freqs)
            cos, sin = (jnp.cos(ang), jnp.sin(ang))
            xr = xh.reshape(xh.shape[:-1] + (d // 2, 2))
            x0, x1 = (xr[..., 0], xr[..., 1])
            rot = jnp.stack([x0 * cos - x1 * sin, x0 * sin + x1 * cos], axis=-1)
            return rot.reshape(xh.shape)

        def _attention(x, Wq, Wkva, Wkvb, Wo):
            b, t, _ = x.shape
            q = (x @ Wq).reshape(b, t, H, D).transpose(0, 2, 1, 3)
            ckv = x @ Wkva
            kv_latent, k_rope = (ckv[:, :, :R], ckv[:, :, R:])
            kv = (kv_latent @ Wkvb).reshape(b, t, H, NOPE).transpose(0, 2, 1, 3)
            k_rope = jnp.broadcast_to(k_rope[:, None, :, :], (b, H, t, ROPE))
            q_nope, q_rope = (q[..., :NOPE], q[..., NOPE:])
            q = jnp.concatenate([q_nope, _rope(q_rope)], axis=-1)
            k = jnp.concatenate([kv, _rope(k_rope)], axis=-1)
            v = jnp.concatenate([kv, jnp.zeros_like(k_rope)], axis=-1)
            att = jnp.einsum('bhqd,bhkd->bhqk', q, k) / jnp.sqrt(jnp.float32(D))
            mask = jnp.tril(jnp.ones((t, t), dtype=bool))
            att = jnp.where(mask, att, jnp.float32(-jnp.inf))
            att = jax.nn.softmax(att, axis=-1)
            y = jnp.einsum('bhqk,bhkd->bhqd', att, v)
            y = y.transpose(0, 2, 1, 3).reshape(b, t, H * D)
            return y @ Wo

        def _experts(x_flat, Wg, Wu, Wd):
            g = jax.nn.silu(jnp.einsum('nc,eci->nei', x_flat, Wg))
            u = jnp.einsum('nc,eci->nei', x_flat, Wu)
            return jnp.einsum('nei,eic->nec', g * u, Wd)

        def _moe(x, Wgate, expert_bias, Wg, Wu, Wd, sWg, sWu, sWd):
            b, t, c = x.shape
            xf = x.reshape(-1, c)
            shared = jnp.mean(_experts(xf, sWg, sWu, sWd), axis=1)
            logits = xf @ Wgate + expert_bias
            probs = jax.nn.softmax(logits, axis=-1)
            topk_p, topk_i = jax.lax.top_k(probs, K)
            topk_p = topk_p / jnp.sum(topk_p, axis=-1, keepdims=True)
            comb = jnp.sum(jax.nn.one_hot(topk_i, E, dtype=xf.dtype) * topk_p[..., None], axis=1)
            routed = jnp.einsum('ne,nec->nc', comb, _experts(xf, Wg, Wu, Wd))
            return (shared + routed).reshape(b, t, c)
        key = jax.random.key(seed)
        ks = jax.random.split(key, 16)
        w = lambda k, shp: jax.random.normal(k, shp, dtype=jnp.float32) * 0.02
        return {'x': jax.random.normal(ks[0], (B, T, C), dtype=jnp.float32), 'w_ln1': jnp.ones((C,), jnp.float32), 'Wq': w(ks[1], (C, H * D)), 'Wkva': w(ks[2], (C, R + ROPE)), 'Wkvb': w(ks[3], (R, H * NOPE)), 'Wo': w(ks[4], (H * D, C)), 'w_ln2': jnp.ones((C,), jnp.float32), 'Wgate': w(ks[5], (C, E)), 'expert_bias': jnp.zeros((E,), jnp.float32), 'Wg': w(ks[6], (E, C, I)), 'Wu': w(ks[7], (E, C, I)), 'Wd': w(ks[8], (E, I, C)), 'sWg': w(ks[9], (S, C, I)), 'sWu': w(ks[10], (S, C, I)), 'sWd': w(ks[11], (S, I, C))}
    _L0_ffn_in = _L0_ffn_setup()
    _d = {'L0_attn_x': _L0_attn_in['x'], 'L0_attn_W_spin': _L0_attn_in['W_spin'], 'L0_attn_b_spin': _L0_attn_in['b_spin'], 'L0_attn_W_global': _L0_attn_in['W_global'], 'L0_attn_W_J': _L0_attn_in['W_J'], 'L0_attn_beta': _L0_attn_in['beta'], 'L0_ffn_w_ln1': _L0_ffn_in['w_ln1'], 'L0_ffn_Wq': _L0_ffn_in['Wq'], 'L0_ffn_Wkva': _L0_ffn_in['Wkva'], 'L0_ffn_Wkvb': _L0_ffn_in['Wkvb'], 'L0_ffn_Wo': _L0_ffn_in['Wo'], 'L0_ffn_w_ln2': _L0_ffn_in['w_ln2'], 'L0_ffn_Wgate': _L0_ffn_in['Wgate'], 'L0_ffn_expert_bias': _L0_ffn_in['expert_bias'], 'L0_ffn_Wg': _L0_ffn_in['Wg'], 'L0_ffn_Wu': _L0_ffn_in['Wu'], 'L0_ffn_Wd': _L0_ffn_in['Wd'], 'L0_ffn_sWg': _L0_ffn_in['sWg'], 'L0_ffn_sWu': _L0_ffn_in['sWu'], 'L0_ffn_sWd': _L0_ffn_in['sWd']}
    _x0 = _d['L0_attn_x']
    _d['L0_attn_x'] = jax.random.normal(jax.random.fold_in(jax.random.key(seed), 1), (1, 2048, 128), dtype=_x0.dtype)
    del _x0
    return _d

def reference(L0_attn_x, L0_attn_W_spin, L0_attn_b_spin, L0_attn_W_global, L0_attn_W_J, L0_attn_beta, L0_ffn_w_ln1, L0_ffn_Wq, L0_ffn_Wkva, L0_ffn_Wkvb, L0_ffn_Wo, L0_ffn_w_ln2, L0_ffn_Wgate, L0_ffn_expert_bias, L0_ffn_Wg, L0_ffn_Wu, L0_ffn_Wd, L0_ffn_sWg, L0_ffn_sWu, L0_ffn_sWd):

    def _L0_attn_ref(x, W_spin, b_spin, W_global, W_J, beta):
        import jax, jax.numpy as jnp
        import numpy as np
        B, N, D_IN, D_OUT = (4, 256, 128, 128)
        s = jnp.einsum('bni,oi->bno', x, W_spin) + b_spin
        mean_field = jnp.mean(s, axis=1, keepdims=True)
        global_influence = jnp.einsum('bmd,od->bmo', mean_field, W_global)
        energy_fields = jnp.einsum('bnd,od->bno', s, W_J)
        scale = 1.0 / jnp.sqrt(jnp.float32(s.shape[2]))
        scores = jnp.einsum('bnd,bmd->bnm', energy_fields, s) * scale
        affinities = jax.nn.softmax(scores, axis=-1)
        local_field = jnp.einsum('bnm,bmd->bnd', affinities, s)
        return jnp.tanh(beta * (s + global_influence + local_field))

    def _L0_ffn_ref(x, w_ln1, Wq, Wkva, Wkvb, Wo, w_ln2, Wgate, expert_bias, Wg, Wu, Wd, sWg, sWu, sWd):
        import jax, jax.numpy as jnp
        import numpy as np
        B, T, C = (2, 256, 128)
        H, D = (16, 64)
        CR = 8
        R = C // CR
        ROPE = D // 2
        NOPE = D - ROPE
        E, K, I, S = (8, 2, 64, 1)
        THETA = 100000.0
        EPS = 1e-05

        def _rmsnorm(x, w):
            rms = jnp.sqrt(jnp.mean(x * x, axis=-1, keepdims=True) + EPS)
            return w * (x / rms)

        def _rope(xh):
            d = xh.shape[-1]
            t = jnp.arange(xh.shape[2], dtype=jnp.float32)
            freqs = 1.0 / THETA ** (jnp.arange(0, d, 2, dtype=jnp.float32) / d)
            ang = jnp.outer(t, freqs)
            cos, sin = (jnp.cos(ang), jnp.sin(ang))
            xr = xh.reshape(xh.shape[:-1] + (d // 2, 2))
            x0, x1 = (xr[..., 0], xr[..., 1])
            rot = jnp.stack([x0 * cos - x1 * sin, x0 * sin + x1 * cos], axis=-1)
            return rot.reshape(xh.shape)

        def _attention(x, Wq, Wkva, Wkvb, Wo):
            b, t, _ = x.shape
            q = (x @ Wq).reshape(b, t, H, D).transpose(0, 2, 1, 3)
            ckv = x @ Wkva
            kv_latent, k_rope = (ckv[:, :, :R], ckv[:, :, R:])
            kv = (kv_latent @ Wkvb).reshape(b, t, H, NOPE).transpose(0, 2, 1, 3)
            k_rope = jnp.broadcast_to(k_rope[:, None, :, :], (b, H, t, ROPE))
            q_nope, q_rope = (q[..., :NOPE], q[..., NOPE:])
            q = jnp.concatenate([q_nope, _rope(q_rope)], axis=-1)
            k = jnp.concatenate([kv, _rope(k_rope)], axis=-1)
            v = jnp.concatenate([kv, jnp.zeros_like(k_rope)], axis=-1)
            att = jnp.einsum('bhqd,bhkd->bhqk', q, k) / jnp.sqrt(jnp.float32(D))
            mask = jnp.tril(jnp.ones((t, t), dtype=bool))
            att = jnp.where(mask, att, jnp.float32(-jnp.inf))
            att = jax.nn.softmax(att, axis=-1)
            y = jnp.einsum('bhqk,bhkd->bhqd', att, v)
            y = y.transpose(0, 2, 1, 3).reshape(b, t, H * D)
            return y @ Wo

        def _experts(x_flat, Wg, Wu, Wd):
            g = jax.nn.silu(jnp.einsum('nc,eci->nei', x_flat, Wg))
            u = jnp.einsum('nc,eci->nei', x_flat, Wu)
            return jnp.einsum('nei,eic->nec', g * u, Wd)

        def _moe(x, Wgate, expert_bias, Wg, Wu, Wd, sWg, sWu, sWd):
            b, t, c = x.shape
            xf = x.reshape(-1, c)
            shared = jnp.mean(_experts(xf, sWg, sWu, sWd), axis=1)
            logits = xf @ Wgate + expert_bias
            probs = jax.nn.softmax(logits, axis=-1)
            topk_p, topk_i = jax.lax.top_k(probs, K)
            topk_p = topk_p / jnp.sum(topk_p, axis=-1, keepdims=True)
            comb = jnp.sum(jax.nn.one_hot(topk_i, E, dtype=xf.dtype) * topk_p[..., None], axis=1)
            routed = jnp.einsum('ne,nec->nc', comb, _experts(xf, Wg, Wu, Wd))
            return (shared + routed).reshape(b, t, c)
        x = x + _attention(_rmsnorm(x, w_ln1), Wq, Wkva, Wkvb, Wo)
        residual = x
        xn = _rmsnorm(x, w_ln2)
        x_out = _moe(xn, Wgate, expert_bias, Wg, Wu, Wd, sWg, sWu, sWd)
        return residual + x_out
    x = L0_attn_x
    x = x + _L0_attn_ref(_layernorm(x, axis=-1), L0_attn_W_spin, L0_attn_b_spin, L0_attn_W_global, L0_attn_W_J, L0_attn_beta)
    x = x + _L0_ffn_ref(_layernorm(x, axis=-1), L0_ffn_w_ln1, L0_ffn_Wq, L0_ffn_Wkva, L0_ffn_Wkvb, L0_ffn_Wo, L0_ffn_w_ln2, L0_ffn_Wgate, L0_ffn_expert_bias, L0_ffn_Wg, L0_ffn_Wu, L0_ffn_Wd, L0_ffn_sWg, L0_ffn_sWu, L0_ffn_sWd)
    return x

_drawn_inputs = setup_inputs


def setup_inputs(seed=0):
    import zlib

    import numpy as np

    out = dict(_drawn_inputs(seed))
    spreads = {'L0_ffn_w_ln1': (1.0, 0.6), 'L0_ffn_w_ln2': (1.0, 0.6), 'L0_ffn_expert_bias': (0.0, 0.8)}
    factors = {'L0_attn_W_J': 4.852,
     'L0_ffn_Wq': 8.0,
     'L0_ffn_Wkva': 8.0,
     'L0_ffn_Wkvb': 8.0,
     'L0_ffn_Wo': 8.0,
     'L0_ffn_Wgate': 8.0,
     'L0_ffn_Wg': 8.0,
     'L0_ffn_Wu': 8.0,
     'L0_ffn_Wd': 8.0,
     'L0_ffn_sWg': 8.0,
     'L0_ffn_sWu': 8.0,
     'L0_ffn_sWd': 8.0}
    for name, (base, spread) in spreads.items():
        noise = np.random.default_rng([zlib.crc32(name.encode()), seed]).standard_normal(out[name].shape)
        drawn = base * np.exp(spread * noise) if base else spread * noise
        out[name] = jnp.asarray(drawn.astype(out[name].dtype))
    for name, factor in factors.items():
        out[name] = (out[name] * factor).astype(out[name].dtype)
    return out
```

```python
from contextlib import ExitStack

import concourse.bass as bass
from concourse import mybir
from concourse.alu_op_type import AluOpType as ALU

F32 = mybir.dt.float32
F32R = mybir.dt.float32r
U32 = mybir.dt.uint32
ACT = mybir.ActivationFunctionType
AX = mybir.AxisListType

P = 128
N = 2048
NB = N // P
GB = 4
NG = NB // GB
BANK = 512
H = 16
HG = 4
LAT = 16
ROPE = 32
NOPE = 32
KD = LAT + ROPE
VW = 32
E = 8
EI = 64
EPS = 1e-5
BIG = 1e30
SCALE_A = 1.0 / float(P) ** 0.5
SCALE_B = 0.125
SLOTS = 8
ST_BANKS = 3


def plan_attention():

    def prepare(i):
        return [("xr", i), ("qp", i, 0), ("qp", i, 1)] + [("tk", i)] + [("tq", i, g) for g in range(4)]

    def maxima(i):
        return [("mx", i, h, c) for h in range(H) for c in range(i // 4 + 1)]

    plan = prepare(0) + prepare(1) + maxima(0) + [("nm", 0)]
    late = []
    slot = 0
    waiting = None
    for i in range(NB):
        quads = [(g, q) for g in range(4) for q in range(i // 4 + 1)]
        count = len(quads)
        early = max(1, (count * 7) // 10)
        prep = prepare(i + 2) if i + 2 < NB else []
        maxi = maxima(i + 1) if i + 1 < NB else []
        for n, (g, q) in enumerate(quads):
            plan.append(("st", i, g, q))
            if waiting:
                plan.append(waiting)
                _, wi, wg, wq = waiting
                if wq == wi // 4:
                    late.append((slot + 1, ("yt", wi, wg)))
                    if wg == 3:
                        late += [(slot + 2, ("yn", wi)), (slot + 3, ("yo", wi))]
            waiting = ("av", i, g, q)
            plan += maxi[min(n, early) * len(maxi) // early:min(n + 1, early) * len(maxi) // early]
            if n + 1 == early and maxi:
                plan.append(("nm", i + 1))
            plan += prep[n * len(prep) // count:(n + 1) * len(prep) // count]
            plan += [s for at, s in late if at == slot]
            late = [x for x in late if x[0] > slot]
            slot += 1
    plan.append(waiting)
    plan += [s for _, s in late]
    plan += [("yt", NB - 1, 3), ("yn", NB - 1), ("yo", NB - 1)]
    return plan


def build(nc, x, w_spin, b_spin, w_global, w_j, beta, w_ln1, w_ln2, w_nope, w_all, w_kv, w_out,
          w_gate, e_bias, w_eg, w_eu, w_ed, w_sd, ident, future, iota, cos, sin, out):
    plan = plan_attention()
    empties = {"xr": "act", "qp": "dve", "tq": "act", "tk": "act", "nm": "act", "yt": "dve", "yn": "act", "yo": "dve"}
    turn, emptied, tally = {}, [], {"act": 0, "dve": 0}
    max_no, tile_no, av_no = {}, {}, {}
    for step in plan:
        if step[0] in empties:
            who = empties[step[0]]
            tally[who] += 1
            turn[step] = len(emptied)
            emptied.append((who, tally[who]))
        elif step[0] == "mx":
            max_no[step] = len(max_no)
        elif step[0] == "st":
            _, i, g, q = step
            for j in range(4 * q, min(4 * q + 4, i + 1)):
                tile_no[i, g, j] = len(tile_no)
        elif step[0] == "av":
            av_no[step] = len(av_no)
    av_of_tile = {}
    for (_, i, g, q), a in av_no.items():
        for j in range(4 * q, min(4 * q + 4, i + 1)):
            av_of_tile[tile_no[i, g, j]] = a

    ctx = ExitStack()
    with ctx:
        def sb(name, shape, dt=F32):
            return ctx.enter_context(nc.sbuf_tensor(name, shape, dt))

        def sem(name):
            return ctx.enter_context(nc.semaphore(name))

        psum = ctx.enter_context(nc.psum_tensor("psum", [P, 8, BANK], F32))

        wsp = sb("wsp", [P, P]); wgl = sb("wgl", [P, P]); wj = sb("wj", [P, P])
        bsp = sb("bsp", [P, 1]); bet = sb("bet", [P, 1]); ln1 = sb("ln1", [P, 1]); ln2 = sb("ln2", [P, 1])
        wnope = sb("wnope", [P, 4, P]); wall = sb("wall", [P, H + 1, KD]); wkv = sb("wkv", [P, 4, LAT])
        wout = sb("wout", [P, 4, P]); wgate = sb("wgate", [P, E]); ebias = sb("ebias", [P, E])
        weg = sb("weg", [P, E + 1, EI]); weu = sb("weu", [P, E + 1, EI])
        wed = sb("wed", [P, E // 2, P]); wsd = sb("wsd", [EI, P])
        idn = sb("idn", [P, P]); fut = sb("fut", [P, P]); iot = sb("iot", [P, E])
        cs = sb("cs", [P, NB, ROPE]); sn = sb("sn", [P, NB, ROPE])
        idr = sb("idr", [P, P], F32R); futr = sb("futr", [P, P], F32R)
        half_neg = sb("half_neg", [P, NB])
        kv_diag = sb("kv_diag", [P, 4, HG * LAT])
        wvo = sb("wvo", [P, 2, P])

        X = sb("X", [P, NB, P]); X1 = X; Y = sb("Y", [P, NB, P]); YR = sb("YR", [P, NB, P])
        stats = sb("stats", [P, NB, 6]); mom = sb("mom", [P, NB, 2]); var_e = sb("var_e", [P, NB]); rstd = sb("rstd", [P, NB])
        xn = YR
        xnT = sb("xnT", [P, N]); sT = sb("sT", [P, N]); s_tok = sb("s_tok", [P, NB, P]); sg = Y
        mean_parts = sb("mean_parts", [P, NG]); mean_sum = sb("mean_sum", [P, 1]); mean_b = sb("mean_b", [P, P]); gi = sb("gi", [P, P])
        eT = sb("eT", [P, 2, BANK])
        region = sb("region", [P, 2 * N + 2 * NB * BANK])
        prob = region[:, 0:2 * N].rearrange("p (a n) -> p a n", a=2)
        probT = region[:, 2 * N:2 * N + 2 * NB * BANK].rearrange("p (a m n) -> p a m n", a=2, m=NB)
        nmax = sb("nmax", [P, NB]); nbias = sb("nbias", [P, NB]); rsum = sb("rsum", [P, NB]); rden = sb("rden", [P, NB])
        oT = sb("oT", [P, BANK]); z = sb("z", [P, BANK]); th = sb("th", [P, BANK])
        stats1 = sb("stats1", [P, NB, 6]); mom1 = sb("mom1", [P, NB, 2])
        ve1 = sb("ve1", [P, NB]); rs1 = sb("rs1", [P, NB]); sq1 = sb("sq1", [P, NB]); ms1 = sb("ms1", [P, NB]); me1 = sb("me1", [P, NB]); rr1 = sb("rr1", [P, NB])

        qT = sb("qT", [P, 3, H * P], F32R)
        kT = sb("kT", [P, 2, N], F32R)
        used = 0

        def take(count):
            nonlocal used
            used += count
            return region[:, used - count:used]

        val = sb("val", [P, NB, VW])
        pb = take(SLOTS * BANK).rearrange("p (s n) -> p s n", s=SLOTS)
        xrT = take(2 * P).rearrange("p (a n) -> p a n", a=2)
        rot1 = take(9 * ROPE).rearrange("p (h d) -> p h d", d=ROPE)
        rot2 = take(9 * ROPE).rearrange("p (h d) -> p h d", d=ROPE)
        qf = take(2 * (H + 1) * KD).rearrange("p (a h d) -> p a h d", a=2, d=KD)
        qs = take(2 * (H + 1) * 2 * KD).rearrange("p (a h c d) -> p a h c d", a=2, c=2, d=KD)
        ks = take(2 * 2 * 2 * KD).rearrange("p (a c r d) -> p a c r d", a=2, c=2, r=2)
        part_max = take(2 * H * 4).rearrange("p (a h c) -> p a h c", a=2, h=H)
        neg_max = take(H)
        acc_s = take(2 * BANK).rearrange("p (a n) -> p a n", a=2)
        ysum = take(H * (LAT + 1)).rearrange("p (h d) -> p h d", h=H)
        yden = take(H)
        ynorm = take(H * LAT).rearrange("p (h d) -> p h d", h=H)
        yT = take(2 * P).rearrange("p (a n) -> p a n", a=2)
        neg_maxT = sb("neg_maxT", [H, P], F32R)
        hid = xnT[:, :].rearrange("p (b c) -> p b c", b=NB)
        stats2 = stats; mom2 = mom
        ms2 = sb("ms2", [P, NB]); r2 = sb("r2", [P, NB])
        xn2 = YR
        xfT = sT
        x1h = s_tok
        used = 0
        logit = take(NB * E).rearrange("p (b e) -> p b e", b=NB)
        lmax = take(NB)
        lshift = take(NB * E).rearrange("p (b e) -> p b e", b=NB)
        pe_ = take(NB * E).rearrange("p (b e) -> p b e", b=NB)
        top = take(NB * E).rearrange("p (b e) -> p b e", b=NB)
        idx = take(NB * E).bitcast(U32).rearrange("p (b e) -> p b e", b=NB)
        idxf = take(NB * 2).rearrange("p (b e) -> p b e", b=NB)
        pick0 = take(NB * E).rearrange("p (b e) -> p b e", b=NB)
        pick1 = take(NB * E).rearrange("p (b e) -> p b e", b=NB)
        pick = take(NB * E).rearrange("p (b e) -> p b e", b=NB)
        chosen = take(NB * E).rearrange("p (b e) -> p b e", b=NB)
        csum = take(NB)
        crec = take(NB)
        comb = take(NB * E).rearrange("p (b e) -> p b e", b=NB)
        tg = take(2 * BANK).rearrange("p (a n) -> p a n", a=2)
        ga = take(2 * BANK).rearrange("p (a n) -> p a n", a=2)
        gu = take(2 * BANK).rearrange("p (a n) -> p a n", a=2)
        hT = take(2 * 5 * BANK).rearrange("p (a k n) -> p a k n", a=2, k=5)
        comb_b = take(NB * E * EI).rearrange("p (b n) -> p b n", b=NB)
        res = take(2 * BANK).rearrange("p (a n) -> p a n", a=2)

        x_in = [sem(f"x_in{t}") for t in range(NG)]; w_in = sem("w_in"); w2_in = sem("w2_in")
        const_set = sem("const_set"); k_one_set = sem("k_one_set"); kv_zero = sem("kv_zero"); kv_placed = sem("kv_placed")
        masks_r = sem("masks_r"); sd_half = sem("sd_half")
        absorb_filled = sem("absorb_filled"); absorb_ready = sem("absorb_ready")
        x_stats = sem("x_stats"); x_mom = sem("x_mom"); x_var = sem("x_var"); x_rstd = sem("x_rstd"); xn_ready = sem("xn_ready")
        xnT_filled = sem("xnT_filled"); xnT_ready = sem("xnT_ready")
        s_filled = sem("s_filled"); s_ready = sem("s_ready"); st_filled = sem("st_filled"); st_ready = sem("st_ready")
        mean_step = sem("mean_step"); gi_filled = sem("gi_filled"); gi_ready = sem("gi_ready"); sg_ready = sem("sg_ready")
        e_filled = sem("e_filled"); e_ready = sem("e_ready")
        sc_filled = sem("sc_filled"); max_found = sem("max_found"); bias_ready = sem("bias_ready"); exp_done = sem("exp_done")
        pT_filled = sem("pT_filled"); pT_ready = sem("pT_ready")
        o_filled = sem("o_filled"); oT_ready = sem("oT_ready"); ot_filled = sem("ot_filled")
        rden_ready = sem("rden_ready"); z_ready = sem("z_ready"); th_ready = sem("th_ready"); x1_ready = sem("x1_ready")
        y_stats = sem("y_stats"); y_mom = sem("y_mom"); y_pool = sem("y_pool"); y_ready = sem("y_ready"); yr_ready = sem("yr_ready")
        filled = sem("filled"); act_emptied = sem("act_emptied"); dve_emptied = sem("dve_emptied")
        rotated = sem("rotated"); qf_ready = sem("qf_ready"); q_high = sem("q_high"); q_split = sem("q_split")
        tile_filled = sem("tile_filled"); tile_exp = sem("tile_exp"); tile_masked = sem("tile_masked"); av_done = sem("av_done")
        acc_emptied = sem("acc_emptied")
        max_filled = sem("max_filled"); max_emptied = sem("max_emptied"); neg_max_ready = sem("neg_max_ready"); max_row_in = sem("max_row_in")
        yden_ready = sem("yden_ready"); ynorm_ready = sem("ynorm_ready")
        h_stats = sem("h_stats"); h_mom = sem("h_mom"); h_pool = sem("h_pool"); xn2_ready = sem("xn2_ready"); x1h_ready = sem("x1h_ready")
        xfT_filled = sem("xfT_filled"); xfT_ready = sem("xfT_ready"); lg_filled = sem("lg_filled")
        route = sem("route"); comb_ready = sem("comb_ready"); lexp_ready = sem("lexp_ready")
        g_filled = sem("g_filled"); u_filled = sem("u_filled"); c_filled = sem("c_filled")
        tanh_done = sem("tanh_done"); ga_done = sem("ga_done"); gu_done = sem("gu_done"); hT_ready = sem("hT_ready")
        d_filled = sem("d_filled"); res_ready = sem("res_ready"); out_done = [sem(f"out_done{t}") for t in range(NG)]

        block = ctx.enter_context(nc.Block())

        x_view = x.rearrange("(b p) c -> p b c", p=P)
        out_view = out.rearrange("(b p) c -> p b c", p=P)
        first_loads = [(wsp, w_spin), (bsp, b_spin), (idn, ident), (wgl, w_global), (wj, w_j), (bet, beta)]
        later_loads = [(ln1, w_ln1), (ln2, w_ln2), (wnope, w_nope), (wall, w_all), (wkv, w_kv), (wout, w_out),
                       (wgate, w_gate), (ebias, e_bias), (weg, w_eg), (weu, w_eu), (wed, w_ed), (wsd, w_sd),
                       (fut, future), (iot, iota), (cs, cos), (sn, sin)]
        W1 = 16 * len(first_loads)
        W2 = 16 * len(later_loads)

        def tokens(t):
            return slice(t * BANK, (t + 1) * BANK)

        def group(t):
            return slice(t * GB, (t + 1) * GB)

        def bank4(b):
            return psum[:, b, :].rearrange("p (a c) -> p a c", a=GB)

        def misc(T):
            return psum[:, 6 + T % 2, :]

        def wait_emptied(eng, T):
            who, count = emptied[T]
            eng.wait_ge(act_emptied if who == "act" else dve_emptied, count)

        pairs = E // 2
        ROUTE_STEPS = 13

        @block.sync
        def _(sp):
            for t in range(NG):
                sp.dma_start(X[:, group(t), :], x_view[:, group(t), :]).then_inc(x_in[t], 16)
                if t == 0:
                    for dst, src in first_loads:
                        sp.dma_start(dst[:], src).then_inc(w_in, 16)
            for dst, src in later_loads:
                sp.dma_start(dst[:], src).then_inc(w2_in, 16)
            for step in plan:
                if step[0] == "nm":
                    i = step[1]
                    wait_emptied(sp, turn[step])
                    sp.dma_start(qT[2 * KD:2 * KD + 1, i % 3, :].bitcast(F32), neg_maxT[:, :].bitcast(F32)).then_inc(max_row_in, 16)
            for t in range(NG):
                sp.wait_ge(res_ready, t + 1)
                sp.dma_start(out_view[:, group(t), :], res[:, t % 2, :].rearrange("p (b c) -> p b c", b=GB)).then_inc(out_done[t], 16)
            for t in range(NG):
                sp.wait_ge(out_done[t], 16)

        @block.tensor
        def _(pe):
            def transpose(dst, src):
                rows = src.shape[0]
                return nc.tensor.transpose(dst, src, idn[0:rows, 0:rows])

            pe.wait_ge(w_in, W1)
            for t in range(NG):
                pe.wait_ge(xn_ready, GB * (t + 1))
                if t >= 2:
                    pe.wait_ge(xnT_ready, t - 1)
                for u in range(GB):
                    last = transpose(psum[:, 4 + t % 2, u * P:(u + 1) * P], xn[:, GB * t + u, :])
                last.then_inc(xnT_filled, 1)
            for t in range(NG):
                pe.wait_ge(xnT_ready, t + 1)
                if t >= 2:
                    pe.wait_ge(s_ready, t - 1)
                nc.tensor.matmul(psum[:, 6 + t % 2, :], wsp[:], xnT[:, tokens(t)], start=True, stop=True).then_inc(s_filled, 1)
            for t in range(NG):
                pe.wait_ge(s_ready, t + 1)
                if t < 2:
                    pe.wait_ge(xnT_ready, NG)
                else:
                    pe.wait_ge(st_ready, t - 1)
                for u in range(GB):
                    last = transpose(psum[:, 4 + t % 2, u * P:(u + 1) * P], sT[:, (GB * t + u) * P:(GB * t + u + 1) * P])
                last.then_inc(st_filled, 1)
            pe.wait_ge(mean_step, 3)
            nc.tensor.matmul(psum[:, 6, 0:P], mean_b[:], wgl[:], start=True, stop=True).then_inc(gi_filled, 1)

            def energy(t):
                pe.wait_ge(s_ready, NG)
                if t >= 2:
                    pe.wait_ge(z_ready, GB * (t - 1))
                elif t == 1:
                    pe.wait_ge(e_ready, 1)
                nc.tensor.matmul(psum[:, 7, :], wj[:], sT[:, tokens(t)], start=True, stop=True).then_inc(e_filled, 1)

            def probs_transposed(n):
                pe.wait_ge(exp_done, n + 1)
                for k in range(4):
                    if 4 * n + k >= 2:
                        pe.wait_ge(pT_ready, 4 * n + k - 1)
                    for m in range(4):
                        last = transpose(psum[:, 4 + k % 2, m * P:(m + 1) * P], prob[:, n % 2, (4 * k + m) * P:(4 * k + m + 1) * P])
                    last.then_inc(pT_filled, 1)

            def local_field(t, m0, m1):
                pe.wait_ge(pT_ready, 16 * (t + 1))
                if t == 0 and m0 == 0:
                    pe.wait_ge(gi_ready, 1)
                if t >= 1 and m0 == 0:
                    pe.wait_ge(oT_ready, t)
                for m in range(m0, m1):
                    last = nc.tensor.matmul(psum[:, 6, :], s_tok[:, m, :], probT[:, t % 2, m, :], start=(m == 0), stop=(m == NB - 1))
                if m1 == NB:
                    last.then_inc(o_filled, 1)

            def local_field_by_tokens(t):
                pe.wait_ge(oT_ready, t + 1)
                pe.wait_ge(e_ready, min(t + 2, NG))
                if t == NG - 1:
                    pe.wait_ge(z_ready, GB * (NG - 1))
                for u in range(GB):
                    last = transpose(psum[:, 7, u * P:(u + 1) * P], oT[:, u * P:(u + 1) * P])
                last.then_inc(ot_filled, 1)

            pe.wait_ge(st_ready, NG)
            pe.wait_ge(s_ready, NG)
            energy(0)
            for t in range(NG):
                for u in range(GB):
                    n = GB * t + u
                    pe.wait_ge(e_ready, t + 1)
                    if n >= 1:
                        pe.wait_ge(exp_done, n)
                    for c in range(4):
                        last = nc.tensor.matmul(psum[:, c, :], eT[:, t % 2, u * P:(u + 1) * P], sT[:, tokens(c)], start=True, stop=True)
                    last.then_inc(sc_filled, 1)
                    if n >= 1:
                        probs_transposed(n - 1)
                    if t >= 1 and u >= 1:
                        local_field(t - 1, (0, 0, 5, 10)[u], (0, 5, 10, 16)[u])
                    if t == 0 and u == 2:
                        energy(1)
                    if t >= 1 and u == 3:
                        local_field_by_tokens(t - 1)
                        if t < NG - 1:
                            energy(t + 1)
            probs_transposed(NB - 1)
            local_field(NG - 1, 0, NB)
            local_field_by_tokens(NG - 1)

            pe.wait_ge(w2_in, W2)
            pe.wait_ge(kv_placed, 16)
            pe.wait_ge(exp_done, NB)
            pe.wait_ge(pT_ready, 4 * NB)
            pe.wait_ge(z_ready, NB)
            for k in range(4):
                last = nc.tensor.matmul(psum[:, 0, k * 64:(k + 1) * 64], wnope[:, k, :], kv_diag[:, k, :], start=True, stop=True)
            last.then_inc(absorb_filled, 1)
            for k in range(4):
                last = nc.tensor.matmul(psum[64 * (k % 2):64 * (k % 2) + 64, 1, (k // 2) * P:(k // 2 + 1) * P], kv_diag[:, k, :],
                                        wout[:, k, :], start=True, stop=True)
            last.then_inc(absorb_filled, 1)
            pe.wait_ge(absorb_ready, 2)
            pe.wait_ge(masks_r, 2)
            pe.wait_ge(const_set, 3)
            pe.wait_ge(k_one_set, 1)

            for step in plan:
                kind, i = step[0], step[1]
                T = turn.get(step)
                if T is not None and T >= 2:
                    wait_emptied(pe, T - 2)
                if kind == "xr":
                    pe.wait_ge(yr_ready, i + 1)
                    transpose(misc(T)[:, 0:P], YR[:, i, :]).then_inc(filled, 1)
                elif kind == "qp":
                    h0, h1 = ((0, 9), (9, H + 1))[step[2]]
                    wait_emptied(pe, turn["xr", i])
                    nc.tensor.matmul(misc(T)[:, 0:(h1 - h0) * KD], xrT[:, i % 2, :], wall[:, h0:h1, :], start=True, stop=True).then_inc(filled, 1)
                elif kind == "tk":
                    pe.wait_ge(q_split, i + 1)
                    for c in range(2):
                        last = transpose(misc(T)[0:2 * KD, c * P:(c + 1) * P], ks[:, i % 2, c, :, :])
                    last.then_inc(filled, 1)
                elif kind == "tq":
                    g = step[2]
                    for m in range(HG):
                        last = transpose(misc(T)[0:2 * KD, m * P:(m + 1) * P], qs[:, i % 2, HG * g + m, :, :])
                    last.then_inc(filled, 1)
                elif kind == "mx":
                    _, _, h, c = step
                    m = max_no[step]
                    if m >= 2:
                        pe.wait_ge(max_emptied, m - 1)
                    wait_emptied(pe, turn["tq", i, h // HG])
                    k0, k1 = c * BANK, min((c + 1) * BANK, (i + 1) * P)
                    diag = k1 == (i + 1) * P
                    last = nc.tensor.matmul(psum[:, 4 + m % 2, 0:k1 - k0], qT[0:2 * KD, i % 3, h * P:(h + 1) * P],
                                            kT[0:2 * KD, 0, k0:k1], start=True, stop=not diag)
                    if diag:
                        last = nc.tensor.matmul(psum[:, 4 + m % 2, k1 - k0 - P:k1 - k0], idr[:], futr[:], start=False, stop=True)
                    last.then_inc(max_filled, 1)
                elif kind == "nm":
                    pe.wait_ge(neg_max_ready, i + 1)
                    transpose(misc(T)[0:H, 0:P], neg_max[:, :]).then_inc(filled, 1)
                elif kind == "st":
                    _, _, g, q = step
                    if g == 0 and q == 0:
                        pe.wait_ge(max_row_in, 16 * (i + 1))
                    for j in range(4 * q, min(4 * q + 4, i + 1)):
                        n = tile_no[i, g, j]
                        if n >= ST_BANKS:
                            pe.wait_ge(tile_exp, n - ST_BANKS + 1)
                        cols = slice(g * BANK, (g + 1) * BANK)
                        nc.tensor.matmul(psum[:, n % ST_BANKS, :], kT[0:2 * KD + 1, 0, j * P:(j + 1) * P], qT[0:2 * KD + 1, i % 3, cols],
                                         start=True, stop=False)
                        nc.tensor.matmul(psum[:, n % ST_BANKS, :], kT[0:2 * KD, 1, j * P:(j + 1) * P], qT[0:2 * KD, i % 3, cols],
                                         start=False, stop=True).then_inc(tile_filled, 1)
                elif kind == "av":
                    _, _, g, q = step
                    unit = 4 * i + g
                    js = range(4 * q, min(4 * q + 4, i + 1))
                    if q == 0 and unit >= 1:
                        pe.wait_ge(acc_emptied, unit)
                    pe.wait_ge(tile_exp, tile_no[i, g, js[-1]] + 1)
                    if js[-1] == i:
                        pe.wait_ge(tile_masked, unit + 1)
                    for j in js:
                        r = 32 * (j % 4)
                        last = nc.tensor.matmul(psum[r:r + VW, 3, :], val[:, j, :], pb[:, tile_no[i, g, j] % SLOTS, :],
                                                start=(j < 4), stop=(j + 4 > i), skip_group_check=True)
                    last.then_inc(av_done, 1)
                elif kind == "yt":
                    g = step[2]
                    rows = 32 * min(4, i + 1)
                    pe.wait_ge(acc_emptied, 4 * i + g + 1)
                    for m in range(HG):
                        last = transpose(misc(T)[:, m * P:m * P + rows], acc_s[0:rows, g % 2, m * P:(m + 1) * P])
                    last.then_inc(filled, 1)
                elif kind == "yn":
                    pe.wait_ge(ynorm_ready, i + 1)
                    for k in range(2):
                        last = transpose(misc(T)[:, k * P:(k + 1) * P], ynorm[:, 8 * k:8 * k + 8, :])
                    last.then_inc(filled, 1)
                elif kind == "yo":
                    wait_emptied(pe, turn["yn", i])
                    for k in range(2):
                        last = nc.tensor.matmul(misc(T)[:, 0:P], yT[:, k, :], wvo[:, k, :], start=(k == 0), stop=(k == 1))
                    last.then_inc(filled, 1)

            T = len(emptied)
            for t in range(NG):
                pe.wait_ge(xn2_ready, GB * (t + 1))
                if t < 2:
                    wait_emptied(pe, T - 2)
                    wait_emptied(pe, T - 1)
                else:
                    pe.wait_ge(xfT_ready, t - 1)
                for u in range(GB):
                    last = transpose(psum[:, 6 + t % 2, u * P:(u + 1) * P], xn2[:, GB * t + u, :])
                last.then_inc(xfT_filled, 1)
            pe.wait_ge(max_emptied, len(max_no))
            pe.wait_ge(tile_exp, len(tile_no))
            for t in range(NG):
                pe.wait_ge(xfT_ready, t + 1)
                for u in range(GB):
                    b = GB * t + u
                    last = nc.tensor.matmul(psum[:, 4, b * E:(b + 1) * E], xfT[:, b * P:(b + 1) * P], wgate[:], start=True, stop=True)
            last.then_inc(lg_filled, 1)

            def up(t, k):
                m = 5 * t + k
                if m >= 2:
                    pe.wait_ge(hT_ready, m - 1)
                rows = P if k < pairs else EI
                es = slice(2 * k, 2 * k + 2) if k < pairs else slice(E, E + 1)
                nc.tensor.matmul(psum[0:rows, m % 2, :], weg[:, es, :], xfT[:, tokens(t)], start=True, stop=True).then_inc(g_filled, 1)
                nc.tensor.matmul(psum[0:rows, 2 + m % 2, :], weu[:, es, :], xfT[:, tokens(t)], start=True, stop=True).then_inc(u_filled, 1)
                if k < pairs:
                    pe.wait_ge(comb_ready, t + 1)
                    for u in range(GB):
                        weights = comb_b[:, GB * t + u, 2 * k * EI:(2 * k + 2) * EI]
                        last = transpose(psum[:, 4 + m % 2, u * P:(u + 1) * P], weights)
                    last.then_inc(c_filled, 1)

            def down(t):
                pe.wait_ge(hT_ready, 5 * (t + 1))
                pe.wait_ge(sd_half, 2)
                if t < 2:
                    pe.wait_ge(xfT_ready, NG)
                else:
                    pe.wait_ge(res_ready, t - 1)
                for u in range(GB):
                    for k in range(5):
                        rows = P if k < pairs else EI
                        last = nc.tensor.matmul(psum[:, 6 + t % 2, u * P:(u + 1) * P], hT[0:rows, t % 2, k, u * P:(u + 1) * P],
                                                wed[:, k, :] if k < pairs else wsd[:], start=(k == 0), stop=(k == 4))
                last.then_inc(d_filled, 1)

            for t in range(NG):
                for k in range(5):
                    up(t, k)
                    if t >= 1 and k == 1:
                        down(t - 1)
            down(NG - 1)

        @block.scalar
        def _(act):
            act.wait_ge(w_in, W1)
            for t in range(NG):
                act.wait_ge(xnT_filled, t + 1)
                nc.scalar.copy(xnT[:, tokens(t)], psum[:, 4 + t % 2, :]).then_inc(xnT_ready, 1)
            for t in range(NG):
                act.wait_ge(s_filled, t + 1)
                nc.scalar.activation(sT[:, tokens(t)], psum[:, 6 + t % 2, :], ACT.Identity, bias=bsp[:],
                                     accum_out=mean_parts[:, t:t + 1]).then_inc(s_ready, 1)

            def energy(t):
                act.wait_ge(e_filled, t + 1)
                nc.scalar.copy(eT[:, t % 2, :], psum[:, 7, :]).then_inc(e_ready, 1)

            def probs_transposed(n):
                t, u = n // GB, n % GB
                if u == 0 and t >= 2:
                    act.wait_ge(o_filled, t - 1)
                for k in range(4):
                    act.wait_ge(pT_filled, 4 * n + k + 1)
                    nc.scalar.copy(probT[:, t % 2, 4 * k:4 * k + 4, u * P:(u + 1) * P], bank4(4 + k % 2)).then_inc(pT_ready, 1)

            def field_tanh(t):
                act.wait_ge(z_ready, GB * (t + 1))
                if t >= 1:
                    act.wait_ge(x1_ready, t)
                nc.scalar.activation(th[:], z[:], ACT.Tanh, scale=bet[:]).then_inc(th_ready, 1)

            energy(0)
            for t in range(NG):
                for u in range(GB):
                    n = GB * t + u
                    if n >= 1:
                        probs_transposed(n - 1)
                    act.wait_ge(bias_ready, n + 1)
                    nc.scalar.activation(prob[:, n % 2, :], psum[:, 0:4, :], ACT.Exp, bias=nbias[:, n:n + 1], scale=SCALE_A,
                                         accum_out=rsum[:, n:n + 1]).then_inc(exp_done, 1)
                    if t == 0 and u == 2:
                        energy(1)
                    if t >= 1 and u == 3:
                        field_tanh(t - 1)
                        if t < NG - 1:
                            energy(t + 1)
            probs_transposed(NB - 1)
            field_tanh(NG - 1)

            act.wait_ge(absorb_filled, 1)
            nc.scalar.copy(wall[:, 0:H, 0:LAT], psum[:, 0, 0:H * LAT].rearrange("p (h r) -> p h r", h=H)).then_inc(absorb_ready, 1)
            act.wait_ge(absorb_filled, 2)
            nc.scalar.copy(wvo[:], psum[:, 1, 0:2 * P].rearrange("p (k c) -> p k c", k=2)).then_inc(absorb_ready, 1)
            act.wait_ge(w2_in, W2)

            for step in plan:
                kind, i = step[0], step[1]
                T = turn.get(step)
                if T is not None and emptied[T][0] == "act":
                    act.wait_ge(filled, T + 1)
                if kind == "xr":
                    nc.scalar.activation(xrT[:, i % 2, :], misc(T)[:, 0:P], ACT.Copy, scale=ln1[:]).then_inc(act_emptied, 1)
                elif kind == "tk":
                    nc.scalar.copy(kT[0:2 * KD, 0, i * P:(i + 1) * P], misc(T)[0:2 * KD, 0:P])
                    nc.scalar.copy(kT[0:2 * KD, 1, i * P:(i + 1) * P], misc(T)[0:2 * KD, P:2 * P]).then_inc(act_emptied, 1)
                elif kind == "tq":
                    g = step[2]
                    nc.scalar.copy(qT[0:2 * KD, i % 3, g * BANK:(g + 1) * BANK], misc(T)[0:2 * KD, :]).then_inc(act_emptied, 1)
                elif kind == "nm":
                    if i >= 1:
                        act.wait_ge(max_row_in, 16 * i)
                    nc.scalar.copy(neg_maxT[:, :], misc(T)[0:H, 0:P]).then_inc(act_emptied, 1)
                elif kind == "st":
                    _, _, g, q = step
                    for j in range(4 * q, min(4 * q + 4, i + 1)):
                        n = tile_no[i, g, j]
                        act.wait_ge(tile_filled, n + 1)
                        if n >= SLOTS:
                            act.wait_ge(av_done, av_of_tile[n - SLOTS] + 1)
                        nc.scalar.activation(pb[:, n % SLOTS, :], psum[:, n % ST_BANKS, :], ACT.Exp, scale=SCALE_B).then_inc(tile_exp, 1)
                elif kind == "av":
                    _, _, g, q = step
                    if q == i // 4:
                        unit = 4 * i + g
                        rows = 32 * min(4, i + 1)
                        act.wait_ge(av_done, av_no[step] + 1)
                        if unit >= 2:
                            act.wait_ge(filled, turn["yt", (unit - 2) // 4, (unit - 2) % 4] + 1)
                        nc.scalar.copy(acc_s[0:rows, g % 2, :], psum[0:rows, 3, :]).then_inc(acc_emptied, 1)
                elif kind == "yn":
                    nc.scalar.copy(yT[:], misc(T)[:, 0:2 * P].rearrange("p (k c) -> p k c", k=2)).then_inc(act_emptied, 1)

            for t in range(NG):
                act.wait_ge(xfT_filled, t + 1)
                nc.scalar.activation(xfT[:, tokens(t)], psum[:, 6 + t % 2, :], ACT.Copy, scale=ln2[:]).then_inc(xfT_ready, 1)
            act.wait_ge(route, 3)
            nc.scalar.activation(pe_, lshift, ACT.Exp).then_inc(lexp_ready, 1)
            for t in range(NG):
                for k in range(5):
                    m = 5 * t + k
                    rows = P if k < pairs else EI
                    act.wait_ge(g_filled, m + 1)
                    if m >= 2:
                        act.wait_ge(ga_done, m - 1)
                    nc.scalar.activation(tg[0:rows, m % 2, :], psum[0:rows, m % 2, :], ACT.Tanh, scale=0.5).then_inc(tanh_done, 1)

        @block.vector
        def _(dve):
            nc.vector.memset(kT[2 * KD:2 * KD + 1, 0, :].bitcast(F32), 1.0).then_inc(k_one_set, 1)
            for b in range(NB):
                if b % GB == 0:
                    dve.wait_ge(x_in[b // GB], 16)
                nc.vector.bn_stats(stats[:, b, :], X[:, b, :]).then_inc(x_stats, 1)
            for b in range(NB):
                dve.wait_ge(x_stats, b + 1)
                nc.vector.bn_aggr(mom[:, b, :], stats[:, b, :]).then_inc(x_mom, 1)
            dve.wait_ge(x_rstd, 1)
            for b in range(NB):
                nc.vector.tensor_scalar(xn[:, b, :], X[:, b, :], mom[:, b, 0:1], rstd[:, b:b + 1], ALU.subtract, ALU.mult).then_inc(xn_ready, 1)
            for t in range(NG):
                dve.wait_ge(st_filled, t + 1)
                nc.vector.tensor_copy(s_tok[:, group(t), :], bank4(4 + t % 2)).then_inc(st_ready, 1)
            dve.wait_ge(s_ready, NG)
            nc.vector.tensor_reduce(mean_sum[:], mean_parts[:], AX.X, ALU.add).then_inc(mean_step, 1)
            dve.wait_ge(mean_step, 1)
            nc.vector.tensor_scalar(mean_sum[:], mean_sum[:], 1.0 / N, None, ALU.mult).then_inc(mean_step, 1)
            dve.wait_ge(mean_step, 2)
            nc.vector.tensor_copy(mean_b[:], mean_sum[:].to_broadcast([P, P])).then_inc(mean_step, 1)
            dve.wait_ge(gi_filled, 1)
            nc.vector.tensor_copy(gi[:], psum[:, 6, 0:P]).then_inc(gi_ready, 1)

            dve.wait_ge(w2_in, W2)
            dve.wait_ge(kv_zero, 1)
            for k in range(4):
                for m in range(HG):
                    nc.vector.tensor_copy(kv_diag[NOPE * m:NOPE * m + NOPE, k, LAT * m:LAT * m + LAT],
                                          wkv[NOPE * m:NOPE * m + NOPE, k, :]).then_inc(kv_placed, 1)
            nc.vector.tensor_copy(idr[:], idn[:]).then_inc(masks_r, 1)
            nc.vector.tensor_copy(futr[:], fut[:]).then_inc(masks_r, 1)
            nc.vector.tensor_scalar(wed[:], wed[:], 0.5, None, ALU.mult).then_inc(sd_half, 1)
            nc.vector.tensor_scalar(wsd[:], wsd[:], 0.5, None, ALU.mult).then_inc(sd_half, 1)

            def field(t):
                dve.wait_ge(o_filled, t + 1)
                if t >= 1:
                    dve.wait_ge(ot_filled, t)
                nc.vector.tensor_copy(oT[:], psum[:, 6, :]).then_inc(oT_ready, 1)
                dve.wait_ge(exp_done, GB * (t + 1))
                nc.vector.reciprocal(rden[:, group(t)], rsum[:, group(t)]).then_inc(rden_ready, 1)
                dve.wait_ge(rden_ready, t + 1)
                dve.wait_ge(sg_ready, NG)
                if t >= 1:
                    dve.wait_ge(th_ready, t)
                dve.wait_ge(ot_filled, t + 1)
                for u in range(GB):
                    b = GB * t + u
                    nc.vector.scalar_tensor_tensor(z[:, u * P:(u + 1) * P], psum[:, 7, u * P:(u + 1) * P], rden[:, b:b + 1],
                                                   sg[:, b, :], ALU.mult, ALU.add).then_inc(z_ready, 1)

            def norm1(t):
                dve.wait_ge(x1_ready, t + 1)
                for b in range(GB * t, GB * t + GB):
                    nc.vector.bn_stats(stats1[:, b, :], X1[:, b, :]).then_inc(y_stats, 1)
                for b in range(GB * t, GB * t + GB):
                    dve.wait_ge(y_stats, b + 1)
                    nc.vector.bn_aggr(mom1[:, b, :], stats1[:, b, :]).then_inc(y_mom, 1)
                dve.wait_ge(y_pool, 5 * t + 2)
                dve.wait_ge(y_mom, GB * (t + 1))
                for b in range(GB * t, GB * t + GB):
                    nc.vector.tensor_scalar(Y[:, b, :], X1[:, b, :], mom1[:, b, 0:1], rs1[:, b:b + 1], ALU.subtract, ALU.mult).then_inc(y_ready, 1)

            for n in range(NB):
                t, u = n // GB, n % GB
                dve.wait_ge(sc_filled, n + 1)
                nc.vector.tensor_reduce(nmax[:, n:n + 1], psum[:, 0:4, :], AX.XY, ALU.max, negate=True).then_inc(max_found, 1)
                dve.wait_ge(max_found, n + 1)
                nc.vector.tensor_scalar(nbias[:, n:n + 1], nmax[:, n:n + 1], SCALE_A, None, ALU.mult).then_inc(bias_ready, 1)
                if t >= 1 and u == 3:
                    field(t - 1)
                if t >= 2 and u == 1:
                    norm1(t - 2)
            norm1(NG - 2)
            field(NG - 1)
            norm1(NG - 1)

            rot = 0
            for step in plan:
                kind, i = step[0], step[1]
                T = turn.get(step)
                if kind == "qp":
                    half = step[2]
                    h0, h1 = ((0, 9), (9, H + 1))[half]
                    k = h1 - h0
                    src = misc(T)[:, 0:k * KD].rearrange("p (h d) -> p h d", d=KD)
                    lo, hi = src[:, :, LAT:LAT + ROPE // 2], src[:, :, LAT + ROPE // 2:KD]
                    cos_b = cs[:, i:i + 1, :].to_broadcast([P, k, ROPE])
                    sin_lo = sn[:, i:i + 1, 0:ROPE // 2].to_broadcast([P, k, ROPE // 2])
                    sin_hi = sn[:, i:i + 1, ROPE // 2:ROPE].to_broadcast([P, k, ROPE // 2])
                    dve.wait_ge(filled, T + 1)
                    if i >= 2:
                        dve.wait_ge(q_split, i - 1)
                    if 2 * i + half >= 1:
                        dve.wait_ge(qf_ready, 2 * i + half)
                    nc.vector.tensor_tensor(rot1[:, 0:k, :], src[:, :, LAT:KD], cos_b, ALU.mult).then_inc(rotated, 1)
                    nc.vector.tensor_tensor(rot2[:, 0:k, 0:ROPE // 2], hi, sin_lo, ALU.mult).then_inc(rotated, 1)
                    nc.vector.tensor_tensor(rot2[:, 0:k, ROPE // 2:ROPE], lo, sin_hi, ALU.mult).then_inc(rotated, 1)
                    nc.vector.tensor_copy(qf[:, i % 2, h0:h1, 0:LAT], src[:, :, 0:LAT]).then_inc(dve_emptied, 1)
                    rot += 3
                    dve.wait_ge(rotated, rot)
                    nc.vector.tensor_tensor(qf[:, i % 2, h0:h1, LAT:KD], rot1[:, 0:k, :], rot2[:, 0:k, :], ALU.add).then_inc(qf_ready, 1)
                elif kind == "mx":
                    _, _, h, c = step
                    m = max_no[step]
                    w = min((c + 1) * BANK, (i + 1) * P) - c * BANK
                    dve.wait_ge(max_filled, m + 1)
                    if i >= 2:
                        dve.wait_ge(neg_max_ready, i - 1)
                    nc.vector.tensor_reduce(part_max[:, i % 2, h, c:c + 1], psum[:, 4 + m % 2, 0:w], AX.X, ALU.max).then_inc(max_emptied, 1)
                elif kind == "nm":
                    dve.wait_ge(max_emptied, max_no["mx", i, H - 1, i // 4] + 1)
                    if i >= 1:
                        dve.wait_ge(filled, turn["nm", i - 1] + 1)
                    nc.vector.tensor_reduce(neg_max[:, :], part_max[:, i % 2, :, 0:i // 4 + 1], AX.X, ALU.max, negate=True).then_inc(neg_max_ready, 1)
                elif kind == "yt":
                    g = step[2]
                    tiles = min(4, i + 1)
                    if i >= 1:
                        dve.wait_ge(ynorm_ready, i)
                    src = misc(T)[:, :].rearrange("p (m t d) -> p m d t", m=HG, t=4)[:, :, 0:LAT + 1, 0:tiles]
                    dve.wait_ge(filled, T + 1)
                    nc.vector.tensor_reduce(ysum[:, HG * g:HG * g + HG, :], src, AX.X, ALU.add).then_inc(dve_emptied, 1)
                elif kind == "yn":
                    wait_emptied(dve, turn["yt", i, 3])
                    nc.vector.reciprocal(yden, ysum[:, :, LAT]).then_inc(yden_ready, 1)
                    dve.wait_ge(yden_ready, i + 1)
                    if i >= 1:
                        dve.wait_ge(filled, turn["yn", i - 1] + 1)
                    nc.vector.tensor_tensor(ynorm, ysum[:, :, 0:LAT], yden.unsqueeze(2).to_broadcast([P, H, LAT]), ALU.mult).then_inc(ynorm_ready, 1)
                elif kind == "yo":
                    dve.wait_ge(filled, T + 1)
                    nc.vector.tensor_tensor(hid[:, i, :], misc(T)[:, 0:P], Y[:, i, :], ALU.add).then_inc(dve_emptied, 1)
                    wait_emptied(dve, T)
                    nc.vector.bn_stats(stats2[:, i, :], hid[:, i, :]).then_inc(h_stats, 1)
                    dve.wait_ge(h_stats, i + 1)
                    nc.vector.bn_aggr(mom2[:, i, :], stats2[:, i, :]).then_inc(h_mom, 1)

            steps = 0

            def then(ins):
                nonlocal steps
                steps += 1
                ins.then_inc(route, 1)
                dve.wait_ge(route, steps)

            dve.wait_ge(lg_filled, 1)
            then(nc.vector.tensor_tensor(logit, psum[:, 4, 0:NB * E].rearrange("p (b e) -> p b e", b=NB),
                                         ebias[:].unsqueeze(1).to_broadcast([P, NB, E]), ALU.add))
            then(nc.vector.tensor_reduce(lmax, logit, AX.X, ALU.max))
            then(nc.vector.tensor_tensor(lshift, logit, lmax.unsqueeze(2).to_broadcast([P, NB, E]), ALU.subtract))
            dve.wait_ge(lexp_ready, 1)
            for b in range(NB):
                last = nc.vector.max(top[:, b, :], pe_[:, b, :])
            then(last)
            for b in range(NB):
                last = nc.vector.max_index(idx[:, b, :], top[:, b, :], pe_[:, b, :])
            then(last)
            then(nc.vector.tensor_copy(idxf, idx[:, :, 0:2]))
            iota_b = iot[:].unsqueeze(1).to_broadcast([P, NB, E])
            then(nc.vector.tensor_tensor(pick0, iota_b, idxf[:, :, 0:1].to_broadcast([P, NB, E]), ALU.is_equal))
            then(nc.vector.tensor_tensor(pick1, iota_b, idxf[:, :, 1:2].to_broadcast([P, NB, E]), ALU.is_equal))
            then(nc.vector.tensor_tensor(pick, pick0, pick1, ALU.add))
            then(nc.vector.tensor_tensor(chosen, pick, pe_, ALU.mult))
            then(nc.vector.tensor_reduce(csum, chosen, AX.X, ALU.add))
            then(nc.vector.reciprocal(crec, csum))
            then(nc.vector.tensor_tensor(comb, chosen, crec.unsqueeze(2).to_broadcast([P, NB, E]), ALU.mult))
            assert steps == ROUTE_STEPS

            def finish(t):
                dve.wait_ge(d_filled, t + 1)
                dve.wait_ge(x1h_ready, 1)
                if t >= 2:
                    dve.wait_ge(out_done[t - 2], 16)
                nc.vector.tensor_tensor(res[:, t % 2, :].rearrange("p (b c) -> p b c", b=GB), bank4(6 + t % 2), x1h[:, group(t), :],
                                        ALU.add).then_inc(res_ready, 1)

            for t in range(NG):
                for k in range(5):
                    m = 5 * t + k
                    rows = P if k < pairs else EI
                    dve.wait_ge(tanh_done, m + 1)
                    nc.vector.scalar_tensor_tensor(ga[0:rows, m % 2, :], tg[0:rows, m % 2, :], 1.0, psum[0:rows, m % 2, :],
                                                   ALU.add, ALU.mult).then_inc(ga_done, 1)
                    dve.wait_ge(ga_done, m + 1)
                    dve.wait_ge(u_filled, m + 1)
                    if t >= 2 and k == 0:
                        dve.wait_ge(d_filled, t - 1)
                    if k < pairs:
                        nc.vector.tensor_tensor(gu[0:rows, m % 2, :], ga[0:rows, m % 2, :], psum[0:rows, 2 + m % 2, :], ALU.mult).then_inc(gu_done, 1)
                        dve.wait_ge(gu_done, 4 * t + k + 1)
                        dve.wait_ge(c_filled, 4 * t + k + 1)
                        nc.vector.tensor_tensor(hT[:, t % 2, k, :], gu[:, m % 2, :], psum[:, 4 + m % 2, :], ALU.mult).then_inc(hT_ready, 1)
                    else:
                        nc.vector.tensor_tensor(hT[0:rows, t % 2, k, :], ga[0:rows, m % 2, :], psum[0:rows, 2 + m % 2, :], ALU.mult).then_inc(hT_ready, 1)
                    if t >= 1 and k == 2:
                        finish(t - 1)
            finish(NG - 1)

        @block.gpsimd
        def _(pool):
            nc.gpsimd.memset(half_neg[:], -0.5).then_inc(const_set, 1)
            nc.gpsimd.memset(val[:], 0.0).then_inc(const_set, 1)
            pool.wait_ge(const_set, 2)
            nc.gpsimd.memset(val[:, :, LAT:LAT + 1], 1.0).then_inc(const_set, 1)
            nc.gpsimd.memset(kv_diag[:], 0.0).then_inc(kv_zero, 1)
            pool.wait_ge(x_mom, NB)
            nc.gpsimd.tensor_scalar(var_e[:], mom[:, :, 1], EPS, None, ALU.add).then_inc(x_var, 1)
            pool.wait_ge(x_var, 1)
            nc.gpsimd.tensor_tensor(rstd[:], var_e[:], half_neg[:], ALU.pow).then_inc(x_rstd, 1)
            pool.wait_ge(gi_ready, 1)
            for t in range(NG):
                nc.gpsimd.tensor_tensor(sg[:, group(t), :], s_tok[:, group(t), :], gi[:].unsqueeze(1).to_broadcast([P, GB, P]), ALU.add).then_inc(sg_ready, 1)
            for t in range(NG):
                g = group(t)
                pool.wait_ge(th_ready, t + 1)
                nc.gpsimd.tensor_tensor(X1[:, g, :], X[:, g, :], th[:].rearrange("p (b c) -> p b c", b=GB), ALU.add).then_inc(x1_ready, 1)
                pool.wait_ge(y_mom, GB * (t + 1))
                nc.gpsimd.tensor_scalar(ve1[:, g], mom1[:, g, 1], EPS, None, ALU.add).then_inc(y_pool, 1)
                pool.wait_ge(y_pool, 5 * t + 1)
                nc.gpsimd.tensor_tensor(rs1[:, g], ve1[:, g], half_neg[:, 0:GB], ALU.pow).then_inc(y_pool, 1)
                pool.wait_ge(y_pool, 5 * t + 2)
                nc.gpsimd.tensor_tensor(sq1[:, g], rs1[:, g], rs1[:, g], ALU.mult).then_inc(y_pool, 1)
                pool.wait_ge(y_pool, 5 * t + 3)
                nc.gpsimd.tensor_tensor(ms1[:, g], sq1[:, g], mom1[:, g, 1], ALU.mult).then_inc(y_pool, 1)
                pool.wait_ge(y_pool, 5 * t + 4)
                nc.gpsimd.tensor_scalar(me1[:, g], ms1[:, g], EPS, None, ALU.add).then_inc(y_pool, 1)
                pool.wait_ge(y_pool, 5 * t + 5)
                nc.gpsimd.tensor_tensor(rr1[:, g], me1[:, g], half_neg[:, 0:GB], ALU.pow).then_inc(x_rstd, 1)
                pool.wait_ge(x_rstd, t + 2)
                pool.wait_ge(y_ready, GB * (t + 1))
                for b in range(GB * t, GB * t + GB):
                    nc.gpsimd.tensor_scalar(YR[:, b, :], Y[:, b, :], rr1[:, b:b + 1], None, ALU.mult).then_inc(yr_ready, 1)

            highs = 0
            for step in plan:
                kind, i = step[0], step[1]
                if kind == "qp" and step[2] == 1:
                    a = i % 2
                    pool.wait_ge(qf_ready, 2 * (i + 1))
                    if i >= 2:
                        pool.wait_ge(filled, turn["tq", i - 2, 3] + 1)
                    high = qs[:, a, :, 0, :]
                    nc.gpsimd.tensor_copy(high.bitcast(F32R), qf[:, a, :, :]).then_inc(q_high, 1)
                    pool.wait_ge(q_high, 2 * i + 1)
                    nc.gpsimd.tensor_tensor(qs[:, a, :, 1, :].bitcast(F32R), qf[:, a, :, :], high, ALU.subtract).then_inc(q_high, 1)
                    nc.gpsimd.tensor_copy(val[:, i, 0:LAT], qf[:, a, H, 0:LAT])
                    pool.wait_ge(q_high, 2 * i + 2)
                    for r in range(2):
                        last = nc.gpsimd.tensor_copy(ks[:, a, :, r, :], qs[:, a, H, :, :])
                    last.then_inc(q_split, 1)
                elif kind == "st" and step[3] == i // 4:
                    g = step[2]
                    n = tile_no[i, g, i]
                    pool.wait_ge(tile_exp, n + 1)
                    tile = pb[:, n % SLOTS, :].rearrange("p (h q) -> p h q", h=HG)
                    nc.gpsimd.affine_select(out=tile, in_=tile, compare_op=ALU.is_ge, fill=0.0, base=0,
                                            pattern=[[0, HG], [1, P]], channel_multiplier=-1).then_inc(tile_masked, 1)

            pool.wait_ge(h_mom, NB)
            nc.gpsimd.tensor_tensor(ms2[:], mom2[:, :, 0], mom2[:, :, 0], ALU.mult).then_inc(h_pool, 1)
            pool.wait_ge(h_pool, 1)
            nc.gpsimd.tensor_tensor(ms2[:], ms2[:], mom2[:, :, 1], ALU.add).then_inc(h_pool, 1)
            pool.wait_ge(h_pool, 2)
            nc.gpsimd.tensor_scalar(ms2[:], ms2[:], EPS, None, ALU.add).then_inc(h_pool, 1)
            pool.wait_ge(h_pool, 3)
            nc.gpsimd.tensor_tensor(r2[:], ms2[:], half_neg[:], ALU.pow).then_inc(h_pool, 1)
            pool.wait_ge(h_pool, 4)
            for b in range(NB):
                nc.gpsimd.tensor_scalar(xn2[:, b, :], hid[:, b, :], r2[:, b:b + 1], None, ALU.mult).then_inc(xn2_ready, 1)
            nc.gpsimd.tensor_tensor(x1h[:], X1[:], hid, ALU.add).then_inc(x1h_ready, 1)
            pool.wait_ge(route, ROUTE_STEPS)
            for t in range(NG):
                wide = comb_b[:, group(t), :].rearrange("p b (e i) -> p (b e) i", e=E)
                narrow = comb[:, group(t), :].rearrange("p b e -> p (b e)").unsqueeze(2).to_broadcast([P, GB * E, EI])
                nc.gpsimd.tensor_copy(wide, narrow).then_inc(comb_ready, 1)


_OUT = [((1, 2048, 128), "float32")]


def kernel(**inputs):
    import numpy as _np
    import concourse.bacc as _bacc
    from concourse import mybir as _mybir
    from concourse.bass_utils import run_bass_kernel_spmd as _run

    a = {k: _np.asarray(v) for k, v in inputs.items()}
    wq = a["L0_ffn_Wq"].reshape(P, H, 64)
    wkva = a["L0_ffn_Wkva"]
    pairs_first = _np.concatenate([_np.arange(0, ROPE, 2), _np.arange(1, ROPE, 2)])
    w_all = _np.zeros((P, H + 1, KD), _np.float32)
    w_all[:, :H, LAT:] = wq[:, :, NOPE + pairs_first]
    w_all[:, H, :LAT] = wkva[:, :LAT]
    w_all[:, H, LAT:] = wkva[:, LAT + pairs_first]
    by_quarter = lambda w: w.reshape(4, P, -1).transpose(1, 0, 2)
    w_nope = by_quarter(wq[:, :, :NOPE].transpose(1, 2, 0).reshape(H * NOPE, P))
    w_kv = by_quarter(a["L0_ffn_Wkvb"].T)
    w_out = by_quarter(a["L0_ffn_Wo"].reshape(H, 64, P)[:, :NOPE].reshape(H * NOPE, P))
    with_shared = lambda w, s: _np.concatenate([w, s]).transpose(1, 0, 2)
    freqs = (_np.float32(1.0) / _np.float32(100000.0) ** (_np.arange(0, ROPE, 2, dtype=_np.float32) / _np.float32(ROPE))).astype(_np.float32)
    ang = _np.outer(_np.arange(N, dtype=_np.float32), freqs).astype(_np.float32)
    c, s = _np.cos(ang), _np.sin(ang)
    by_block = lambda t: t.reshape(NB, P, ROPE).transpose(1, 0, 2)
    cos = by_block(_np.concatenate([c, c], 1))
    sin = by_block(_np.concatenate([-s, s], 1))
    column = lambda v: v.reshape(P, 1)
    arrays = {
        "x": a["L0_attn_x"].reshape(N, P),
        "w_spin": a["L0_attn_W_spin"].T, "b_spin": column(a["L0_attn_b_spin"]), "w_global": a["L0_attn_W_global"].T,
        "w_j": a["L0_attn_W_J"].T, "beta": _np.broadcast_to(a["L0_attn_beta"], (P, 1)),
        "w_ln1": column(a["L0_ffn_w_ln1"]), "w_ln2": column(a["L0_ffn_w_ln2"]),
        "w_nope": w_nope, "w_all": w_all, "w_kv": w_kv, "w_out": w_out,
        "w_gate": a["L0_ffn_Wgate"], "e_bias": _np.broadcast_to(a["L0_ffn_expert_bias"], (P, E)),
        "w_eg": with_shared(a["L0_ffn_Wg"], a["L0_ffn_sWg"]), "w_eu": with_shared(a["L0_ffn_Wu"], a["L0_ffn_sWu"]),
        "w_ed": a["L0_ffn_Wd"].reshape(E // 2, P, P).transpose(1, 0, 2), "w_sd": a["L0_ffn_sWd"].reshape(EI, P),
        "ident": _np.eye(P, dtype=_np.float32), "future": _np.triu(_np.full((P, P), -BIG, _np.float32), 1),
        "iota": _np.broadcast_to(_np.arange(E, dtype=_np.float32), (P, E)), "cos": cos, "sin": sin,
    }
    nc = _bacc.Bacc("TRN2", target_bir_lowering=False, num_devices=1)
    maps, args = {}, []
    for name, v in arrays.items():
        v = _np.ascontiguousarray(v)
        maps[f"in_{name}"] = v
        args.append(nc.dram_tensor(f"in_{name}", v.shape, _mybir.dt.from_np(v.dtype), kind="ExternalInput").ap())
    args.append(nc.dram_tensor("out_0", (N, P), _mybir.dt.float32, kind="ExternalOutput").ap())
    build(nc, *args)
    r = _run(nc, [maps], core_ids=[0])
    return r.results[0]["out_0"].reshape(_OUT[0][0])
```

```python
from contextlib import ExitStack

import concourse.bass as bass
from concourse import mybir
from concourse.alu_op_type import AluOpType as ALU

F32 = mybir.dt.float32
F32R = mybir.dt.float32r
U32 = mybir.dt.uint32
ACT = mybir.ActivationFunctionType
AX = mybir.AxisListType

P = 128
N = 2048
NB = N // P
GB = 4
NG = NB // GB
BANK = 512
H = 16
HG = 4
LAT = 16
ROPE = 32
NOPE = 32
KD = LAT + ROPE
VW = 32
E = 8
EI = 64
EPS = 1e-5
BIG = 1e30
SCALE_A = 1.0 / float(P) ** 0.5
SCALE_B = 0.125
SLOTS = 16
AV_LAG = 3
Y_LAG = 3
NM_LEAD = 6
ST_BANKS = 3


def key_blocks(i):
    return [i] + list(range(i))


def plan_layers():

    def prepare(i):
        return [("xr", i), ("qp", i, 0), ("qp", i, 1), ("tk", i)] + [("tq", i, g) for g in range(4)]

    def maxima(i):
        return [("mx", i, h, c) for h in range(H) for c in range(i // 4 + 1)]

    def experts(t):
        steps = [("hx", t), ("lg", t), ("lx", t), ("rt", t)]
        for k in range(5):
            steps += [("eg", t, k), ("eu", t, k)] + ([("ec", t, k)] if k < 4 else [])
        return steps + [("ed", t)]

    plan = [("xr", 0), ("lf", 0), ("qp", 0, 0), ("qp", 0, 1), ("lf", 1), ("xr", 1), ("lf", 2), ("lf", 3), ("lt",)]
    plan += prepare(0)[3:] + [("lh",), ("qp", 1, 0), ("qp", 1, 1)] + maxima(0) + [("nm", 0), ("ln",)] + prepare(1)[3:]
    late = []
    slot = 0
    side = []
    for i in range(NB):
        tiles = [(g, j) for j in key_blocks(i) for g in range(4)]
        count = len(tiles)
        y_lag = min(Y_LAG, i + 1)
        early = max(1, min(count - NM_LEAD, count * 9 // 10))
        prep = prepare(i + 2) if i + 2 < NB else []
        maxi = maxima(i + 1) if i + 1 < NB else []
        if i % 4 == 0 and i > 0:
            t, start = i // 4 - 1, slot + AV_LAG + 4 * Y_LAG
            end = slot + 4 * sum(range(i + 1, i + 5)) - 4
            steps = experts(t)
            side = [(start + (end - start) * n // len(steps), step) for n, step in enumerate(steps)]
        for n, (g, j) in enumerate(tiles):
            plan.append(("st", i, g, j))
            if g == 3:
                wait = AV_LAG + (4 if j == i and i > 0 else 0)
                late.append((slot + wait, len(late), ("av", i, j)))
            if n == count - 1:
                for m, kind in enumerate(("yt", "yn", "yo")):
                    late.append((slot + AV_LAG + (m + 1) * y_lag, 99, (kind, i)))
            plan += [x[2] for x in sorted(late) if x[0] <= slot]
            late = [x for x in late if x[0] > slot]
            plan += maxi[min(n, early) * len(maxi) // early:min(n + 1, early) * len(maxi) // early]
            if n + 1 == early and maxi:
                plan.append(("nm", i + 1))
            plan += prep[n * len(prep) // count:(n + 1) * len(prep) // count]
            plan += [step for at, step in side if at == slot]
            slot += 1
    return plan + [x[2] for x in sorted(late)] + experts(NG - 1)


def build(nc, x, w_spin, b_spin, w_global, w_j, beta, w_ln1, w_ln2, w_nope, w_all, w_kv, w_out,
          w_gate, e_bias, w_eg, w_eu, w_ed, w_sd, ident, future, iota, cos, sin, out):
    plan = plan_layers()
    empties = {"lt": "dve", "xr": "act", "qp": "dve", "tq": "act", "tk": "act", "nm": "act", "yt": "dve", "yn": "act", "yo": "dve",
               "hx": "act", "lg": "dve", "eg": "act", "eu": "dve", "ec": "dve", "ed": "dve"}
    turn, emptied, tally = {}, [], {"act": 0, "dve": 0}
    max_no, tile_no, av_no = {}, {}, {}
    for step in plan:
        if step[0] in empties:
            who = empties[step[0]]
            tally[who] += 1
            turn[step] = len(emptied)
            emptied.append((who, tally[who]))
        elif step[0] == "mx":
            max_no[step] = len(max_no)
        elif step[0] == "st":
            tile_no[step[1:]] = len(tile_no)
        elif step[0] == "av":
            av_no[step] = len(av_no)
    av_order = {}
    for _, i, j in av_no:
        av_order.setdefault(i, []).append(j)
    tile_keys = {n: key for key, n in tile_no.items()}

    def av_count(n):
        i, _, j = tile_keys[n]
        return av_no["av", i, j] + 1

    def chunk(i, c):
        k0, k1 = c * BANK, min((c + 1) * BANK, (i + 1) * P)
        return k0, k1, (i * P - k0 if k1 == (i + 1) * P else k1 - k0)

    ctx = ExitStack()
    with ctx:
        def sb(name, shape, dt=F32):
            return ctx.enter_context(nc.sbuf_tensor(name, shape, dt))

        def sem(name):
            return ctx.enter_context(nc.semaphore(name))

        psum = ctx.enter_context(nc.psum_tensor("psum", [P, 8, BANK], F32))

        wsp = sb("wsp", [P, P]); wgl = sb("wgl", [P, P]); wj = sb("wj", [P, P])
        bsp = sb("bsp", [P, 1]); bet = sb("bet", [P, 1]); ln1 = sb("ln1", [P, 1]); ln2 = sb("ln2", [P, 1])
        wnope = sb("wnope", [P, 4, P]); wall = sb("wall", [P, H + 1, KD]); wkv = sb("wkv", [P, 4, LAT])
        wout = sb("wout", [P, 4, P]); wgate = sb("wgate", [P, E]); ebias = sb("ebias", [P, E])
        weg = sb("weg", [P, E + 1, EI]); weu = sb("weu", [P, E + 1, EI])
        wed = sb("wed", [P, E // 2, P]); wsd = sb("wsd", [EI, P])
        idn = sb("idn", [P, P]); fut = sb("fut", [P, P]); iot = sb("iot", [P, E])
        cs = sb("cs", [P, NB, ROPE]); sn = sb("sn", [P, NB, ROPE])
        idr = sb("idr", [P, P], F32R)
        half_neg = sb("half_neg", [P, NB])
        kv_diag = sb("kv_diag", [P, 4, HG * LAT])
        wvo = sb("wvo", [P, 2, P])

        X = sb("X", [P, NB, P]); X1 = X; Y = sb("Y", [P, NB, P]); YR = sb("YR", [P, NB, P])
        stats = sb("stats", [P, NB, 6]); mom = sb("mom", [P, NB, 2]); var_e = sb("var_e", [P, NB]); rstd = sb("rstd", [P, NB])
        xn = YR
        xnT = sb("xnT", [P, N]); sT = sb("sT", [P, N]); s_tok = sb("s_tok", [P, NB, P]); sg = Y
        mean_parts = sb("mean_parts", [P, NG]); mean_sum = sb("mean_sum", [P, 1]); mean_b = sb("mean_b", [P, P]); gi = sb("gi", [P, P])
        eT = xnT[:, 0:2 * BANK].rearrange("p (a n) -> p a n", a=2)
        region = sb("region", [P, 2 * N + 2 * NB * BANK])
        prob = region[:, 0:2 * N].rearrange("p (a n) -> p a n", a=2)
        probT = region[:, 2 * N:2 * N + 2 * NB * BANK].rearrange("p (a m n) -> p a m n", a=2, m=NB)
        nmax = sb("nmax", [P, NB]); nbias = sb("nbias", [P, NB]); rsum = sb("rsum", [P, NB]); rden = sb("rden", [P, NB])
        oT = xnT[:, 2 * BANK:3 * BANK]; z = xnT[:, 3 * BANK:4 * BANK]; th = sb("th", [P, BANK])
        stats1 = sb("stats1", [P, NB, 6]); mom1 = sb("mom1", [P, NB, 2])
        ve1 = sb("ve1", [P, NB]); rs1 = sb("rs1", [P, NB]); sq1 = sb("sq1", [P, NB]); ms1 = sb("ms1", [P, NB]); me1 = sb("me1", [P, NB]); rr1 = sb("rr1", [P, NB])

        qT = sb("qT", [P, 3, H * P], F32R)
        kT = sb("kT", [P, 2, N], F32R)
        used = 0

        def take(count):
            nonlocal used
            used += count
            return region[:, used - count:used]

        val = sb("val", [P, NB, VW])
        pb = take(SLOTS * BANK).rearrange("p (s n) -> p s n", s=SLOTS)
        xrT = take(2 * P).rearrange("p (a n) -> p a n", a=2)
        rot1 = take(9 * ROPE).rearrange("p (h d) -> p h d", d=ROPE)
        rot2 = take(9 * ROPE).rearrange("p (h d) -> p h d", d=ROPE)
        qf = take(2 * (H + 1) * KD).rearrange("p (a h d) -> p a h d", a=2, d=KD)
        qs = sb("qs", [P, H + 1, 2, KD], F32R)
        ks = sb("ks", [P, 2, 2, KD], F32R)
        part_max = take(2 * H * 5).rearrange("p (a h c) -> p a h c", a=2, h=H)
        masked = mean_b[:, :]
        neg_max = take(H)
        acc_s = take(BANK)
        yden = take(H).rearrange("p (m g) -> p m g", m=HG)
        ynorm = take(H * LAT).rearrange("p (h d) -> p h d", h=H)
        yT = take(2 * P).rearrange("p (a n) -> p a n", a=2)
        neg_maxT = sb("neg_maxT", [H, P], F32R)
        hid = xnT[:, :].rearrange("p (b c) -> p b c", b=NB)
        stats2 = stats; mom2 = mom
        ms2 = take(NB); r2 = take(NB)
        xn2 = YR
        xfT = sT
        x1h = s_tok
        logit = take(NB * E).rearrange("p (b e) -> p b e", b=NB)
        lmax = take(NB)
        lshift = take(NB * E).rearrange("p (b e) -> p b e", b=NB)
        pe_ = take(NB * E).rearrange("p (b e) -> p b e", b=NB)
        top = take(NB * E).rearrange("p (b e) -> p b e", b=NB)
        idx = take(NB * E).bitcast(U32).rearrange("p (b e) -> p b e", b=NB)
        idxf = take(NB * 2).rearrange("p (b e) -> p b e", b=NB)
        pick0 = take(NB * E).rearrange("p (b e) -> p b e", b=NB)
        pick1 = take(NB * E).rearrange("p (b e) -> p b e", b=NB)
        pick = take(NB * E).rearrange("p (b e) -> p b e", b=NB)
        chosen = take(NB * E).rearrange("p (b e) -> p b e", b=NB)
        csum = take(NB)
        crec = take(NB)
        comb = take(NB * E).rearrange("p (b e) -> p b e", b=NB)
        tg = take(BANK); gs = take(BANK); ga = take(BANK); gu = take(BANK)
        hT = take(5 * BANK).rearrange("p (k n) -> p k n", k=5)
        comb_b = take(GB * E * EI).rearrange("p (b n) -> p b n", b=GB)
        res = take(BANK)

        x_in = [sem(f"x_in{t}") for t in range(NG)]; w_in = sem("w_in"); w2_in = sem("w2_in")
        const_set = sem("const_set"); k_one_set = sem("k_one_set"); kv_zero = sem("kv_zero"); kv_placed = sem("kv_placed")
        idr_ready = sem("idr_ready"); sd_half = sem("sd_half")
        absorb_filled = sem("absorb_filled"); absorb_ready = sem("absorb_ready")
        x_stats = sem("x_stats"); x_mom = sem("x_mom"); x_var = sem("x_var"); x_rstd = sem("x_rstd"); xn_ready = sem("xn_ready")
        xnT_filled = sem("xnT_filled"); xnT_ready = sem("xnT_ready")
        s_filled = sem("s_filled"); s_ready = sem("s_ready"); st_filled = sem("st_filled"); st_ready = sem("st_ready")
        mean_step = sem("mean_step"); gi_filled = sem("gi_filled"); gi_ready = sem("gi_ready"); sg_ready = sem("sg_ready")
        e_filled = sem("e_filled"); e_ready = sem("e_ready")
        sc_filled = sem("sc_filled"); max_found = sem("max_found"); bias_ready = sem("bias_ready"); exp_done = sem("exp_done")
        pT_filled = sem("pT_filled"); pT_ready = sem("pT_ready")
        o_filled = sem("o_filled"); oT_ready = sem("oT_ready"); ot_filled = sem("ot_filled")
        rden_ready = sem("rden_ready"); z_ready = sem("z_ready"); th_ready = sem("th_ready"); x1_ready = sem("x1_ready")
        y_stats = sem("y_stats"); y_mom = sem("y_mom"); y_pool = sem("y_pool"); y_rms = sem("y_rms"); y_ready = sem("y_ready"); yr_ready = sem("yr_ready")
        filled = sem("filled"); act_emptied = sem("act_emptied"); dve_emptied = sem("dve_emptied")
        rotated = sem("rotated"); qf_ready = sem("qf_ready"); q_high = sem("q_high"); q_split = sem("q_split")
        tile_filled = sem("tile_filled"); tile_exp = sem("tile_exp"); tile_masked = sem("tile_masked"); av_done = sem("av_done")
        acc_emptied = sem("acc_emptied")
        max_filled = sem("max_filled"); max_emptied = sem("max_emptied"); neg_max_ready = sem("neg_max_ready"); max_row_in = sem("max_row_in")
        yden_ready = sem("yden_ready")
        h_stats = sem("h_stats"); h_mom = sem("h_mom"); h_pool = sem("h_pool"); xn2_ready = sem("xn2_ready"); x1h_ready = sem("x1h_ready")
        route = sem("route"); comb_ready = sem("comb_ready"); lexp_ready = sem("lexp_ready")
        ga_done = sem("ga_done"); gu_done = sem("gu_done")
        out_done = [sem(f"out_done{t}") for t in range(NG)]

        block = ctx.enter_context(nc.Block())

        x_view = x.rearrange("(b p) c -> p b c", p=P)
        out_view = out.rearrange("(b p) c -> p b c", p=P)
        first_loads = [(idn, ident), (wsp, w_spin), (bsp, b_spin), (wgl, w_global), (wj, w_j), (bet, beta)]
        later_loads = [(ln1, w_ln1), (ln2, w_ln2), (wnope, w_nope), (wall, w_all), (wkv, w_kv), (wout, w_out),
                       (wgate, w_gate), (ebias, e_bias), (weg, w_eg), (weu, w_eu), (wed, w_ed), (wsd, w_sd),
                       (fut, future), (iot, iota), (cs, cos), (sn, sin)]
        W1 = 16 * len(first_loads)
        W2 = 16 * len(later_loads)

        def tokens(t):
            return slice(t * BANK, (t + 1) * BANK)

        def group(t):
            return slice(t * GB, (t + 1) * GB)

        def bank4(b):
            return psum[:, b, :].rearrange("p (a c) -> p a c", a=GB)

        def misc(T):
            return psum[:, 6 + T % 2, :]

        def wait_emptied(eng, T):
            who, count = emptied[T]
            eng.wait_ge(act_emptied if who == "act" else dve_emptied, count)

        pairs = E // 2
        ROUTE_STEPS = 12

        @block.sync
        def _(sp):
            for t in range(NG):
                sp.dma_start(X[:, group(t), :], x_view[:, group(t), :]).then_inc(x_in[t], 16)
                if t == 0:
                    for dst, src in first_loads:
                        sp.dma_start(dst[:], src).then_inc(w_in, 16)
            for dst, src in later_loads:
                sp.dma_start(dst[:], src).then_inc(w2_in, 16)
            for step in plan:
                if step[0] == "nm":
                    i = step[1]
                    wait_emptied(sp, turn[step])
                    sp.dma_start(qT[2 * KD:2 * KD + 1, i % 3, :].bitcast(F32), neg_maxT[:, :].bitcast(F32)).then_inc(max_row_in, 16)
                elif step[0] == "ed":
                    t = step[1]
                    wait_emptied(sp, turn[step])
                    sp.dma_start(out_view[:, group(t), :], res.rearrange("p (b c) -> p b c", b=GB)).then_inc(out_done[t], 16)
            for t in range(NG):
                sp.wait_ge(out_done[t], 16)

        @block.tensor
        def _(pe):
            def transpose(dst, src):
                rows = src.shape[0]
                return nc.tensor.transpose(dst, src, idn[0:rows, 0:rows])

            pe.wait_ge(w2_in, W2)
            pe.wait_ge(kv_placed, 16)
            for k in range(4):
                last = nc.tensor.matmul(psum[:, 0, k * 64:(k + 1) * 64], wnope[:, k, :], kv_diag[:, k, :], start=True, stop=True)
            last.then_inc(absorb_filled, 1)
            for k in range(4):
                last = nc.tensor.matmul(psum[64 * (k % 2):64 * (k % 2) + 64, 1, (k // 2) * P:(k // 2 + 1) * P], kv_diag[:, k, :],
                                        wout[:, k, :], start=True, stop=True)
            last.then_inc(absorb_filled, 1)
            pe.wait_ge(w_in, W1)
            for t in range(NG):
                pe.wait_ge(xn_ready, GB * (t + 1))
                if t >= 2:
                    pe.wait_ge(xnT_ready, t - 1)
                for u in range(GB):
                    last = transpose(psum[:, 4 + t % 2, u * P:(u + 1) * P], xn[:, GB * t + u, :])
                last.then_inc(xnT_filled, 1)
            for t in range(NG):
                pe.wait_ge(xnT_ready, t + 1)
                if t >= 2:
                    pe.wait_ge(s_ready, t - 1)
                nc.tensor.matmul(psum[:, 6 + t % 2, :], wsp[:], xnT[:, tokens(t)], start=True, stop=True).then_inc(s_filled, 1)
            for t in range(NG):
                pe.wait_ge(s_ready, t + 1)
                if t < 2:
                    pe.wait_ge(xnT_ready, NG)
                else:
                    pe.wait_ge(st_ready, t - 1)
                for u in range(GB):
                    last = transpose(psum[:, 4 + t % 2, u * P:(u + 1) * P], sT[:, (GB * t + u) * P:(GB * t + u + 1) * P])
                last.then_inc(st_filled, 1)
            pe.wait_ge(mean_step, 3)
            nc.tensor.matmul(psum[:, 6, 0:P], mean_b[:], wgl[:], start=True, stop=True).then_inc(gi_filled, 1)

            def energy(t):
                pe.wait_ge(s_ready, NG)
                if t >= 2:
                    pe.wait_ge(z_ready, GB * (t - 1))
                elif t == 1:
                    pe.wait_ge(e_ready, 1)
                nc.tensor.matmul(psum[:, 7, :], wj[:], sT[:, tokens(t)], start=True, stop=True).then_inc(e_filled, 1)

            def probs_transposed(n):
                pe.wait_ge(exp_done, n + 1)
                for k in range(4):
                    if 4 * n + k >= 2:
                        pe.wait_ge(pT_ready, 4 * n + k - 1)
                    for m in range(4):
                        last = transpose(psum[:, 4 + k % 2, m * P:(m + 1) * P], prob[:, n % 2, (4 * k + m) * P:(4 * k + m + 1) * P])
                    last.then_inc(pT_filled, 1)

            def local_field(t, m0, m1):
                pe.wait_ge(pT_ready, 16 * (t + 1))
                if t == 0 and m0 == 0:
                    pe.wait_ge(gi_ready, 1)
                if 1 <= t < NG - 1 and m0 == 0:
                    pe.wait_ge(oT_ready, t)
                for m in range(m0, m1):
                    last = nc.tensor.matmul(psum[:, 6 if t < NG - 1 else 3, :], s_tok[:, m, :], probT[:, t % 2, m, :],
                                            start=(m == 0), stop=(m == NB - 1))
                if m1 == NB:
                    last.then_inc(o_filled, 1)

            def local_field_by_tokens(t, dst):
                pe.wait_ge(oT_ready, t + 1)
                if t < NG - 1:
                    pe.wait_ge(e_ready, t + 2)
                for u in range(GB):
                    last = transpose(dst[:, u * P:(u + 1) * P], oT[:, u * P:(u + 1) * P])
                last.then_inc(ot_filled if t < NG - 1 else filled, 1)

            pe.wait_ge(st_ready, NG)
            pe.wait_ge(s_ready, NG)
            energy(0)
            for t in range(NG):
                for u in range(GB):
                    n = GB * t + u
                    pe.wait_ge(e_ready, t + 1)
                    pe.wait_ge(exp_done, n) if n >= 1 else pe.wait_ge(absorb_ready, 2)
                    for c in range(4):
                        last = nc.tensor.matmul(psum[:, c, :], eT[:, t % 2, u * P:(u + 1) * P], sT[:, tokens(c)], start=True, stop=True)
                    last.then_inc(sc_filled, 1)
                    if n >= 1:
                        probs_transposed(n - 1)
                    if t >= 1 and u >= 1:
                        local_field(t - 1, (0, 0, 5, 10)[u], (0, 5, 10, 16)[u])
                    if t == 0 and u == 2:
                        energy(1)
                    if t >= 1 and u == 3:
                        local_field_by_tokens(t - 1, psum[:, 7, :])
                        if t < NG - 1:
                            energy(t + 1)
            probs_transposed(NB - 1)
            pe.wait_ge(exp_done, NB)
            pe.wait_ge(pT_ready, 4 * NB)
            pe.wait_ge(oT_ready, NG - 1)
            pe.wait_ge(z_ready, GB * (NG - 1))
            pe.wait_ge(absorb_ready, 2)
            pe.wait_ge(idr_ready, 1)
            pe.wait_ge(const_set, 3)
            pe.wait_ge(k_one_set, 1)

            for step in plan:
                kind, i = step[0], step[1] if len(step) > 1 else None
                T = turn.get(step)
                if T is not None and T >= 2:
                    wait_emptied(pe, T - 2)
                if kind == "lf":
                    local_field(NG - 1, 4 * i, 4 * i + 4)
                elif kind == "lt":
                    local_field_by_tokens(NG - 1, misc(T))
                elif kind == "xr":
                    pe.wait_ge(yr_ready, i + 1)
                    transpose(misc(T)[:, 0:P], YR[:, i, :]).then_inc(filled, 1)
                elif kind == "qp":
                    h0, h1 = ((0, 9), (9, H + 1))[step[2]]
                    wait_emptied(pe, turn["xr", i])
                    nc.tensor.matmul(misc(T)[:, 0:(h1 - h0) * KD], xrT[:, i % 2, :], wall[:, h0:h1, :], start=True, stop=True).then_inc(filled, 1)
                elif kind == "tk":
                    pe.wait_ge(q_split, i + 1)
                    for c in range(2):
                        last = nc.tensor.matmul(misc(T)[0:2 * KD, c * P:(c + 1) * P], ks[:, c, :, :], idr[:], start=True, stop=True)
                    last.then_inc(filled, 1)
                elif kind == "tq":
                    g = step[2]
                    for m in range(HG):
                        last = nc.tensor.matmul(misc(T)[0:2 * KD, m * P:(m + 1) * P], qs[:, HG * g + m, :, :], idr[:], start=True, stop=True)
                    last.then_inc(filled, 1)
                elif kind == "mx":
                    _, _, h, c = step
                    m = max_no[step]
                    if m >= 2:
                        pe.wait_ge(max_emptied, m - 1)
                    wait_emptied(pe, turn["tq", i, h // HG])
                    k0, k1, _ = chunk(i, c)
                    last = nc.tensor.matmul(psum[:, 4 + m % 2, 0:k1 - k0], qT[0:2 * KD, i % 3, h * P:(h + 1) * P],
                                            kT[0:2 * KD, 0, k0:k1], start=True, stop=True)
                    last.then_inc(max_filled, 1)
                elif kind == "nm":
                    pe.wait_ge(neg_max_ready, i + 1)
                    transpose(misc(T)[0:H, 0:P], neg_max[:, :]).then_inc(filled, 1)
                elif kind == "st":
                    _, _, g, j = step
                    n = tile_no[i, g, j]
                    if g == 0 and j == i:
                        pe.wait_ge(max_row_in, 16 * (i + 1))
                    if n >= ST_BANKS:
                        pe.wait_ge(tile_exp, n - ST_BANKS + 1)
                    cols = slice(g * BANK, (g + 1) * BANK)
                    nc.tensor.matmul(psum[:, n % ST_BANKS, :], kT[0:2 * KD + 1, 0, j * P:(j + 1) * P], qT[0:2 * KD + 1, i % 3, cols],
                                     start=True, stop=False)
                    nc.tensor.matmul(psum[:, n % ST_BANKS, :], kT[0:2 * KD, 1, j * P:(j + 1) * P], qT[0:2 * KD, i % 3, cols],
                                     start=False, stop=True).then_inc(tile_filled, 1)
                elif kind == "av":
                    j = step[2]
                    first, final = j == av_order[i][0], j == av_order[i][-1]
                    if first:
                        pe.wait_ge(acc_emptied, i) if i >= 1 else pe.wait_ge(oT_ready, NG)
                    pe.wait_ge(tile_exp, tile_no[i, 3, j] + 1)
                    if j == i:
                        pe.wait_ge(tile_masked, 4 * (i + 1))
                    for g in range(4):
                        last = nc.tensor.matmul(psum[VW * g:VW * (g + 1), 3, :], val[:, j, :], pb[:, tile_no[i, g, j] % SLOTS, :],
                                                start=first, stop=final)
                    last.then_inc(av_done, 1)
                elif kind == "yt":
                    pe.wait_ge(acc_emptied, i + 1)
                    for m in range(HG):
                        last = transpose(misc(T)[:, m * P:(m + 1) * P], acc_s[:, m * P:(m + 1) * P])
                    last.then_inc(filled, 1)
                elif kind == "yn":
                    wait_emptied(pe, turn["yt", i])
                    for k in range(2):
                        last = transpose(misc(T)[:, k * P:(k + 1) * P], ynorm[:, 8 * k:8 * k + 8, :])
                    last.then_inc(filled, 1)
                elif kind == "yo":
                    wait_emptied(pe, turn["yn", i])
                    for k in range(2):
                        last = nc.tensor.matmul(misc(T)[:, 0:P], yT[:, k, :], wvo[:, k, :], start=(k == 0), stop=(k == 1))
                    last.then_inc(filled, 1)

                elif kind == "hx":
                    pe.wait_ge(xn2_ready, GB * (i + 1))
                    for u in range(GB):
                        last = transpose(misc(T)[:, u * P:(u + 1) * P], xn2[:, GB * i + u, :])
                    last.then_inc(filled, 1)
                elif kind == "lg":
                    wait_emptied(pe, turn["hx", i])
                    for u in range(GB):
                        b = GB * i + u
                        last = nc.tensor.matmul(misc(T)[:, u * E:(u + 1) * E], xfT[:, b * P:(b + 1) * P], wgate[:], start=True, stop=True)
                    last.then_inc(filled, 1)
                elif kind in ("eg", "eu"):
                    k = step[2]
                    rows, es = (P, slice(2 * k, 2 * k + 2)) if k < 4 else (EI, slice(E, E + 1))
                    nc.tensor.matmul(misc(T)[0:rows, :], (weg if kind == "eg" else weu)[:, es, :], xfT[:, tokens(i)],
                                     start=True, stop=True).then_inc(filled, 1)
                elif kind == "ec":
                    k = step[2]
                    pe.wait_ge(comb_ready, i + 1)
                    for u in range(GB):
                        last = transpose(misc(T)[:, u * P:(u + 1) * P], comb_b[:, u, 2 * k * EI:(2 * k + 2) * EI])
                    last.then_inc(filled, 1)
                elif kind == "ed":
                    wait_emptied(pe, turn["eu", i, 4])
                    pe.wait_ge(sd_half, 2)
                    for u in range(GB):
                        for k in range(5):
                            rows = P if k < 4 else EI
                            last = nc.tensor.matmul(misc(T)[:, u * P:(u + 1) * P], hT[0:rows, k, u * P:(u + 1) * P],
                                                    wed[:, k, :] if k < 4 else wsd[:], start=(k == 0), stop=(k == 4))
                    last.then_inc(filled, 1)

        @block.scalar
        def _(act):
            act.wait_ge(w2_in, W2)
            act.wait_ge(absorb_filled, 1)
            nc.scalar.copy(wall[:, 0:H, 0:LAT], psum[:, 0, 0:H * LAT].rearrange("p (h r) -> p h r", h=H)).then_inc(absorb_ready, 1)
            act.wait_ge(absorb_filled, 2)
            nc.scalar.copy(wvo[:], psum[:, 1, 0:2 * P].rearrange("p (k c) -> p k c", k=2)).then_inc(absorb_ready, 1)
            act.wait_ge(w_in, W1)
            for t in range(NG):
                act.wait_ge(xnT_filled, t + 1)
                nc.scalar.copy(xnT[:, tokens(t)], psum[:, 4 + t % 2, :]).then_inc(xnT_ready, 1)
            for t in range(NG):
                act.wait_ge(s_filled, t + 1)
                nc.scalar.activation(sT[:, tokens(t)], psum[:, 6 + t % 2, :], ACT.Identity, bias=bsp[:],
                                     accum_out=mean_parts[:, t:t + 1]).then_inc(s_ready, 1)

            def energy(t):
                act.wait_ge(e_filled, t + 1)
                nc.scalar.copy(eT[:, t % 2, :], psum[:, 7, :]).then_inc(e_ready, 1)

            def probs_transposed(n):
                t, u = n // GB, n % GB
                if u == 0 and t >= 2:
                    act.wait_ge(o_filled, t - 1)
                for k in range(4):
                    act.wait_ge(pT_filled, 4 * n + k + 1)
                    nc.scalar.copy(probT[:, t % 2, 4 * k:4 * k + 4, u * P:(u + 1) * P], bank4(4 + k % 2)).then_inc(pT_ready, 1)

            def field_tanh(t):
                wait_emptied(act, turn["lt",]) if t == NG - 1 else act.wait_ge(z_ready, GB * (t + 1))
                if t >= 1:
                    act.wait_ge(x1_ready, t)
                nc.scalar.activation(th[:], z[:], ACT.Tanh, scale=bet[:]).then_inc(th_ready, 1)

            energy(0)
            for t in range(NG):
                for u in range(GB):
                    n = GB * t + u
                    if n >= 1:
                        probs_transposed(n - 1)
                    act.wait_ge(bias_ready, n + 1)
                    nc.scalar.activation(prob[:, n % 2, :], psum[:, 0:4, :], ACT.Exp, bias=nbias[:, n:n + 1], scale=SCALE_A,
                                         accum_out=rsum[:, n:n + 1]).then_inc(exp_done, 1)
                    if t == 0 and u == 2:
                        energy(1)
                    if t >= 1 and u == 3:
                        field_tanh(t - 1)
                        if t < NG - 1:
                            energy(t + 1)
            probs_transposed(NB - 1)


            for step in plan:
                kind, i = step[0], step[1] if len(step) > 1 else None
                T = turn.get(step)
                if T is not None and emptied[T][0] == "act":
                    act.wait_ge(filled, T + 1)
                if kind == "lh":
                    field_tanh(NG - 1)
                elif kind == "xr":
                    nc.scalar.activation(xrT[:, i % 2, :], misc(T)[:, 0:P], ACT.Copy, scale=ln1[:]).then_inc(act_emptied, 1)
                elif kind == "tk":
                    nc.scalar.copy(kT[0:2 * KD, 0, i * P:(i + 1) * P], misc(T)[0:2 * KD, 0:P])
                    nc.scalar.copy(kT[0:2 * KD, 1, i * P:(i + 1) * P], misc(T)[0:2 * KD, P:2 * P]).then_inc(act_emptied, 1)
                elif kind == "tq":
                    g = step[2]
                    nc.scalar.copy(qT[0:2 * KD, i % 3, g * BANK:(g + 1) * BANK], misc(T)[0:2 * KD, :]).then_inc(act_emptied, 1)
                elif kind == "nm":
                    if i >= 1:
                        act.wait_ge(max_row_in, 16 * i)
                    nc.scalar.copy(neg_maxT[:, :], misc(T)[0:H, 0:P]).then_inc(act_emptied, 1)
                elif kind == "st":
                    n = tile_no[step[1:]]
                    act.wait_ge(tile_filled, n + 1)
                    if n >= SLOTS:
                        act.wait_ge(av_done, av_count(n - SLOTS))
                    nc.scalar.activation(pb[:, n % SLOTS, :], psum[:, n % ST_BANKS, :], ACT.Exp, scale=SCALE_B).then_inc(tile_exp, 1)
                elif kind == "av" and step[2] == av_order[i][-1]:
                    act.wait_ge(av_done, av_no[step] + 1)
                    if i >= 1:
                        act.wait_ge(filled, turn["yt", i - 1] + 1)
                    nc.scalar.copy(acc_s, psum[:, 3, :]).then_inc(acc_emptied, 1)
                elif kind == "yn":
                    nc.scalar.copy(yT[:], misc(T)[:, 0:2 * P].rearrange("p (k c) -> p k c", k=2)).then_inc(act_emptied, 1)

                elif kind == "hx":
                    nc.scalar.activation(xfT[:, tokens(i)], misc(T), ACT.Copy, scale=ln2[:]).then_inc(act_emptied, 1)
                elif kind == "lx":
                    g = group(i)
                    act.wait_ge(route, ROUTE_STEPS * i + 2)
                    nc.scalar.activation(pe_[:, g, :], lshift[:, g, :], ACT.Exp).then_inc(lexp_ready, 1)
                elif kind == "eg":
                    rows = P if step[2] < 4 else EI
                    if 5 * i + step[2] >= 1:
                        act.wait_ge(ga_done, 5 * i + step[2])
                    nc.scalar.activation(tg[0:rows, :], misc(T)[0:rows, :], ACT.Tanh, scale=0.5)
                    nc.scalar.copy(gs[0:rows, :], misc(T)[0:rows, :]).then_inc(act_emptied, 1)

        @block.vector
        def _(dve):
            nc.vector.memset(kT[2 * KD:2 * KD + 1, 0, :].bitcast(F32), 1.0).then_inc(k_one_set, 1)
            for t in range(NG):
                dve.wait_ge(x_in[t], 16)
                for b in range(GB * t, GB * t + GB):
                    nc.vector.bn_stats(stats[:, b, :], X[:, b, :]).then_inc(x_stats, 1)
                for b in range(GB * t, GB * t + GB):
                    dve.wait_ge(x_stats, b + 1)
                    nc.vector.bn_aggr(mom[:, b, :], stats[:, b, :]).then_inc(x_mom, 1)
            dve.wait_ge(w2_in, W2)
            dve.wait_ge(kv_zero, 1)
            for k in range(4):
                for m in range(HG):
                    nc.vector.tensor_copy(kv_diag[NOPE * m:NOPE * m + NOPE, k, LAT * m:LAT * m + LAT],
                                          wkv[NOPE * m:NOPE * m + NOPE, k, :]).then_inc(kv_placed, 1)
            dve.wait_ge(w_in, W1)
            nc.vector.tensor_copy(idr[:], idn[:]).then_inc(idr_ready, 1)
            nc.vector.tensor_scalar(wed[:], wed[:], 0.5, None, ALU.mult).then_inc(sd_half, 1)
            nc.vector.tensor_scalar(wsd[:], wsd[:], 0.5, None, ALU.mult).then_inc(sd_half, 1)
            dve.wait_ge(x_mom, NB)
            for t in range(NG):
                dve.wait_ge(x_rstd, t + 1)
                for b in range(GB * t, GB * t + GB):
                    nc.vector.tensor_scalar(xn[:, b, :], X[:, b, :], mom[:, b, 0:1], rstd[:, b:b + 1], ALU.subtract, ALU.mult).then_inc(xn_ready, 1)
            for t in range(NG):
                dve.wait_ge(st_filled, t + 1)
                nc.vector.tensor_copy(s_tok[:, group(t), :], bank4(4 + t % 2)).then_inc(st_ready, 1)
            dve.wait_ge(s_ready, NG)
            nc.vector.tensor_reduce(mean_sum[:], mean_parts[:], AX.X, ALU.add).then_inc(mean_step, 1)
            dve.wait_ge(mean_step, 1)
            nc.vector.tensor_scalar(mean_sum[:], mean_sum[:], 1.0 / N, None, ALU.mult).then_inc(mean_step, 1)
            dve.wait_ge(mean_step, 2)
            nc.vector.tensor_copy(mean_b[:], mean_sum[:].to_broadcast([P, P])).then_inc(mean_step, 1)
            dve.wait_ge(gi_filled, 1)
            nc.vector.tensor_copy(gi[:], psum[:, 6, 0:P]).then_inc(gi_ready, 1)

            def field_sums(t):
                dve.wait_ge(o_filled, t + 1)
                if t >= 1:
                    dve.wait_ge(ot_filled, t)
                nc.vector.tensor_copy(oT, psum[:, 6 if t < NG - 1 else 3, :]).then_inc(oT_ready, 1)

            def field(t, by_tokens):
                dve.wait_ge(exp_done, GB * (t + 1))
                nc.vector.reciprocal(rden[:, group(t)], rsum[:, group(t)]).then_inc(rden_ready, 1)
                dve.wait_ge(rden_ready, t + 1)
                dve.wait_ge(sg_ready, NG)
                if t >= 1:
                    dve.wait_ge(th_ready, t)
                for u in range(GB):
                    b = GB * t + u
                    last = nc.vector.scalar_tensor_tensor(z[:, u * P:(u + 1) * P], by_tokens[:, u * P:(u + 1) * P], rden[:, b:b + 1],
                                                          sg[:, b, :], ALU.mult, ALU.add)
                    if t < NG - 1 or u < GB - 1:
                        last.then_inc(z_ready, 1)
                return last

            def norm1(t):
                dve.wait_ge(x1_ready, t + 1)
                for b in range(GB * t, GB * t + GB):
                    nc.vector.bn_stats(stats1[:, b, :], X1[:, b, :]).then_inc(y_stats, 1)
                for b in range(GB * t, GB * t + GB):
                    dve.wait_ge(y_stats, b + 1)
                    nc.vector.bn_aggr(mom1[:, b, :], stats1[:, b, :]).then_inc(y_mom, 1)
                dve.wait_ge(y_pool, 5 * t + 2)
                dve.wait_ge(y_mom, GB * (t + 1))
                for b in range(GB * t, GB * t + GB):
                    nc.vector.tensor_scalar(Y[:, b, :], X1[:, b, :], mom1[:, b, 0:1], rs1[:, b:b + 1], ALU.subtract, ALU.mult).then_inc(y_ready, 1)

            for n in range(NB):
                t, u = n // GB, n % GB
                dve.wait_ge(sc_filled, n + 1)
                nc.vector.tensor_reduce(nmax[:, n:n + 1], psum[:, 0:4, :], AX.XY, ALU.max, negate=True).then_inc(max_found, 1)
                dve.wait_ge(max_found, n + 1)
                nc.vector.tensor_scalar(nbias[:, n:n + 1], nmax[:, n:n + 1], SCALE_A, None, ALU.mult).then_inc(bias_ready, 1)
                if t >= 1 and u == 3:
                    field_sums(t - 1)
                    dve.wait_ge(ot_filled, t)
                    field(t - 1, psum[:, 7, :])
                if t >= 2 and u == 1:
                    norm1(t - 2)
            norm1(NG - 2)

            route_steps = []

            def route_step(ins):
                ins.then_inc(route, 1)
                route_steps.append(ins)
                dve.wait_ge(route, len(route_steps))

            rot = 0
            mask_marks = []
            for step in plan:
                kind, i = step[0], step[1] if len(step) > 1 else None
                T = turn.get(step)
                if kind == "lf" and i == 3:
                    field_sums(NG - 1)
                elif kind == "lt":
                    dve.wait_ge(filled, T + 1)
                    field(NG - 1, misc(T)).then_inc(dve_emptied, 1)
                elif kind == "ln":
                    norm1(NG - 1)
                elif kind == "qp":
                    half = step[2]
                    h0, h1 = ((0, 9), (9, H + 1))[half]
                    k = h1 - h0
                    src = misc(T)[:, 0:k * KD].rearrange("p (h d) -> p h d", d=KD)
                    lo, hi = src[:, :, LAT:LAT + ROPE // 2], src[:, :, LAT + ROPE // 2:KD]
                    cos_b = cs[:, i:i + 1, :].to_broadcast([P, k, ROPE])
                    sin_lo = sn[:, i:i + 1, 0:ROPE // 2].to_broadcast([P, k, ROPE // 2])
                    sin_hi = sn[:, i:i + 1, ROPE // 2:ROPE].to_broadcast([P, k, ROPE // 2])
                    dve.wait_ge(filled, T + 1)
                    if i >= 2:
                        dve.wait_ge(q_split, i - 1)
                    if 2 * i + half >= 1:
                        dve.wait_ge(qf_ready, 2 * i + half)
                    nc.vector.tensor_tensor(rot1[:, 0:k, :], src[:, :, LAT:KD], cos_b, ALU.mult).then_inc(rotated, 1)
                    nc.vector.tensor_tensor(rot2[:, 0:k, 0:ROPE // 2], hi, sin_lo, ALU.mult).then_inc(rotated, 1)
                    nc.vector.tensor_tensor(rot2[:, 0:k, ROPE // 2:ROPE], lo, sin_hi, ALU.mult).then_inc(rotated, 1)
                    nc.vector.tensor_copy(qf[:, i % 2, h0:h1, 0:LAT], src[:, :, 0:LAT]).then_inc(dve_emptied, 1)
                    rot += 3
                    dve.wait_ge(rotated, rot)
                    nc.vector.tensor_tensor(qf[:, i % 2, h0:h1, LAT:KD], rot1[:, 0:k, :], rot2[:, 0:k, :], ALU.add).then_inc(qf_ready, 1)
                elif kind == "mx":
                    _, _, h, c = step
                    m = max_no[step]
                    k0, k1, diag = chunk(i, c)
                    dve.wait_ge(max_filled, m + 1)
                    if i >= 2:
                        dve.wait_ge(neg_max_ready, i - 1)
                    scores = psum[:, 4 + m % 2, :]
                    if diag > 0:
                        last = nc.vector.tensor_reduce(part_max[:, i % 2, h, c:c + 1], scores[:, 0:diag], AX.X, ALU.max)
                    if diag < k1 - k0:
                        if len(mask_marks) >= 1:
                            dve.wait_ge(max_emptied, mask_marks[-1])
                        spot = c + 1 if diag > 0 else c
                        last = nc.vector.tensor_tensor_reduce(out=masked, in0=scores[:, diag:k1 - k0], in1=fut[:], scale=1.0, scalar=-BIG,
                                                              op0=ALU.add, op1=ALU.max, accum_out=part_max[:, i % 2, h, spot:spot + 1])
                        mask_marks.append(m + 1)
                    last.then_inc(max_emptied, 1)
                elif kind == "nm":
                    spots = i // 4 + (2 if i % 4 else 1)
                    dve.wait_ge(max_emptied, max_no["mx", i, H - 1, i // 4] + 1)
                    if i >= 1:
                        dve.wait_ge(filled, turn["nm", i - 1] + 1)
                    nc.vector.tensor_reduce(neg_max[:, :], part_max[:, i % 2, :, 0:spots], AX.X, ALU.max, negate=True).then_inc(neg_max_ready, 1)
                elif kind == "yt":
                    src = misc(T)[:, :].rearrange("p (m g d) -> p m g d", m=HG, g=4)
                    dve.wait_ge(filled, T + 1)
                    if i >= 1:
                        dve.wait_ge(filled, turn["yn", i - 1] + 1)
                        wait_emptied(dve, turn["yt", i - 1])
                    nc.vector.reciprocal(yden, src[:, :, :, LAT]).then_inc(yden_ready, 1)
                    dve.wait_ge(yden_ready, i + 1)
                    nc.vector.tensor_tensor(ynorm.rearrange("p (g m) d -> p m g d", g=4), src[:, :, :, 0:LAT],
                                            yden.unsqueeze(3).to_broadcast([P, HG, 4, LAT]), ALU.mult).then_inc(dve_emptied, 1)
                elif kind == "yo":
                    dve.wait_ge(filled, T + 1)
                    nc.vector.tensor_tensor(hid[:, i, :], misc(T)[:, 0:P], Y[:, i, :], ALU.add).then_inc(dve_emptied, 1)
                    wait_emptied(dve, T)
                    nc.vector.bn_stats(stats2[:, i, :], hid[:, i, :]).then_inc(h_stats, 1)
                    dve.wait_ge(h_stats, i + 1)
                    nc.vector.bn_aggr(mom2[:, i, :], stats2[:, i, :]).then_inc(h_mom, 1)
                elif kind == "lg":
                    g = group(i)
                    dve.wait_ge(filled, T + 1)
                    nc.vector.tensor_tensor(logit[:, g, :], misc(T)[:, 0:GB * E].rearrange("p (b e) -> p b e", b=GB),
                                            ebias[:].unsqueeze(1).to_broadcast([P, GB, E]), ALU.add).then_inc(dve_emptied, 1)
                    wait_emptied(dve, T)
                    route_step(nc.vector.tensor_reduce(lmax[:, g], logit[:, g, :], AX.X, ALU.max))
                    route_step(nc.vector.tensor_tensor(lshift[:, g, :], logit[:, g, :], lmax[:, g].unsqueeze(2).to_broadcast([P, GB, E]), ALU.subtract))
                elif kind == "rt":
                    g = group(i)
                    dve.wait_ge(lexp_ready, i + 1)
                    for b in range(GB * i, GB * i + GB):
                        last = nc.vector.max(top[:, b, :], pe_[:, b, :])
                    route_step(last)
                    for b in range(GB * i, GB * i + GB):
                        last = nc.vector.max_index(idx[:, b, :], top[:, b, :], pe_[:, b, :])
                    route_step(last)
                    route_step(nc.vector.tensor_copy(idxf[:, g, :], idx[:, g, 0:2]))
                    iota_b = iot[:].unsqueeze(1).to_broadcast([P, GB, E])
                    route_step(nc.vector.tensor_tensor(pick0[:, g, :], iota_b, idxf[:, g, 0:1].to_broadcast([P, GB, E]), ALU.is_equal))
                    route_step(nc.vector.tensor_tensor(pick1[:, g, :], iota_b, idxf[:, g, 1:2].to_broadcast([P, GB, E]), ALU.is_equal))
                    route_step(nc.vector.tensor_tensor(pick[:, g, :], pick0[:, g, :], pick1[:, g, :], ALU.add))
                    route_step(nc.vector.tensor_tensor(chosen[:, g, :], pick[:, g, :], pe_[:, g, :], ALU.mult))
                    route_step(nc.vector.tensor_reduce(csum[:, g], chosen[:, g, :], AX.X, ALU.add))
                    route_step(nc.vector.reciprocal(crec[:, g], csum[:, g]))
                    route_step(nc.vector.tensor_tensor(comb[:, g, :], chosen[:, g, :], crec[:, g].unsqueeze(2).to_broadcast([P, GB, E]), ALU.mult))
                    assert len(route_steps) == ROUTE_STEPS * (i + 1)
                elif kind == "eu":
                    k = step[2]
                    rows = P if k < 4 else EI
                    wait_emptied(dve, turn["eg", i, k])
                    if 5 * i + k >= 1:
                        wait_emptied(dve, turn["eu", (5 * i + k - 1) // 5, (5 * i + k - 1) % 5])
                    nc.vector.scalar_tensor_tensor(ga[0:rows, :], tg[0:rows, :], 1.0, gs[0:rows, :], ALU.add, ALU.mult).then_inc(ga_done, 1)
                    dve.wait_ge(ga_done, 5 * i + k + 1)
                    dve.wait_ge(filled, T + 1)
                    if k == 4:
                        nc.vector.tensor_tensor(hT[0:rows, k, :], ga[0:rows, :], misc(T)[0:rows, :], ALU.mult).then_inc(dve_emptied, 1)
                    else:
                        if 4 * i + k >= 1:
                            wait_emptied(dve, turn["ec", (4 * i + k - 1) // 4, (4 * i + k - 1) % 4])
                        nc.vector.tensor_tensor(gu, ga, misc(T), ALU.mult).then_inc(dve_emptied, 1)
                elif kind == "ec":
                    k = step[2]
                    wait_emptied(dve, turn["eu", i, k])
                    dve.wait_ge(filled, T + 1)
                    nc.vector.tensor_tensor(hT[:, k, :], gu, misc(T), ALU.mult).then_inc(dve_emptied, 1)
                elif kind == "ed":
                    dve.wait_ge(filled, T + 1)
                    dve.wait_ge(x1h_ready, i + 1)
                    if i >= 1:
                        dve.wait_ge(out_done[i - 1], 16)
                    nc.vector.tensor_tensor(res.rearrange("p (b c) -> p b c", b=GB), misc(T).rearrange("p (b c) -> p b c", b=GB),
                                            x1h[:, group(i), :], ALU.add).then_inc(dve_emptied, 1)

        @block.gpsimd
        def _(pool):
            nc.gpsimd.memset(half_neg[:], -0.5).then_inc(const_set, 1)
            nc.gpsimd.memset(val[:], 0.0).then_inc(const_set, 1)
            pool.wait_ge(const_set, 2)
            nc.gpsimd.memset(val[:, :, LAT:LAT + 1], 1.0).then_inc(const_set, 1)
            nc.gpsimd.memset(kv_diag[:], 0.0).then_inc(kv_zero, 1)
            for t in range(NG):
                g = group(t)
                pool.wait_ge(x_mom, GB * (t + 1))
                nc.gpsimd.tensor_scalar(var_e[:, g], mom[:, g, 1], EPS, None, ALU.add).then_inc(x_var, 1)
                pool.wait_ge(x_var, t + 1)
                nc.gpsimd.tensor_tensor(rstd[:, g], var_e[:, g], half_neg[:, g], ALU.pow).then_inc(x_rstd, 1)
            pool.wait_ge(gi_ready, 1)
            for t in range(NG):
                nc.gpsimd.tensor_tensor(sg[:, group(t), :], s_tok[:, group(t), :], gi[:].unsqueeze(1).to_broadcast([P, GB, P]), ALU.add).then_inc(sg_ready, 1)
            def norm1(t):
                g = group(t)
                pool.wait_ge(th_ready, t + 1)
                nc.gpsimd.tensor_tensor(X1[:, g, :], X[:, g, :], th[:].rearrange("p (b c) -> p b c", b=GB), ALU.add).then_inc(x1_ready, 1)
                pool.wait_ge(y_mom, GB * (t + 1))
                nc.gpsimd.tensor_scalar(ve1[:, g], mom1[:, g, 1], EPS, None, ALU.add).then_inc(y_pool, 1)
                pool.wait_ge(y_pool, 5 * t + 1)
                nc.gpsimd.tensor_tensor(rs1[:, g], ve1[:, g], half_neg[:, 0:GB], ALU.pow).then_inc(y_pool, 1)
                pool.wait_ge(y_pool, 5 * t + 2)
                nc.gpsimd.tensor_tensor(sq1[:, g], rs1[:, g], rs1[:, g], ALU.mult).then_inc(y_pool, 1)
                pool.wait_ge(y_pool, 5 * t + 3)
                nc.gpsimd.tensor_tensor(ms1[:, g], sq1[:, g], mom1[:, g, 1], ALU.mult).then_inc(y_pool, 1)
                pool.wait_ge(y_pool, 5 * t + 4)
                nc.gpsimd.tensor_scalar(me1[:, g], ms1[:, g], EPS, None, ALU.add).then_inc(y_pool, 1)
                pool.wait_ge(y_pool, 5 * t + 5)
                nc.gpsimd.tensor_tensor(rr1[:, g], me1[:, g], half_neg[:, 0:GB], ALU.pow).then_inc(y_rms, 1)
                pool.wait_ge(y_rms, t + 1)
                pool.wait_ge(y_ready, GB * (t + 1))
                for b in range(GB * t, GB * t + GB):
                    nc.gpsimd.tensor_scalar(YR[:, b, :], Y[:, b, :], rr1[:, b:b + 1], None, ALU.mult).then_inc(yr_ready, 1)

            for t in range(NG - 1):
                norm1(t)
            for step in plan:
                kind, i = step[0], step[1] if len(step) > 1 else None
                if kind == "lh":
                    norm1(NG - 1)
                elif kind == "qp" and step[2] == 1:
                    a = i % 2
                    pool.wait_ge(qf_ready, 2 * (i + 1))
                    if i >= 1:
                        pool.wait_ge(filled, turn["tq", i - 1, 3] + 1)
                    nc.gpsimd.tensor_copy(qs[:, :, 0, :], qf[:, a, :, :]).then_inc(q_high, 1)
                    pool.wait_ge(q_high, 2 * i + 1)
                    nc.gpsimd.tensor_tensor(qs[:, :, 1, :], qf[:, a, :, :], qs[:, :, 0, :].bitcast(F32), ALU.subtract).then_inc(q_high, 1)
                    nc.gpsimd.tensor_copy(val[:, i, 0:LAT], qf[:, a, H, 0:LAT])
                    pool.wait_ge(q_high, 2 * i + 2)
                    for r in range(2):
                        last = nc.gpsimd.tensor_copy(ks[:, :, r, :], qs[:, H, :, :].bitcast(F32))
                    last.then_inc(q_split, 1)
                elif kind == "st" and step[3] == i:
                    g = step[2]
                    n = tile_no[i, g, i]
                    pool.wait_ge(tile_exp, n + 1)
                    tile = pb[:, n % SLOTS, :].rearrange("p (h q) -> p h q", h=HG)
                    nc.gpsimd.affine_select(out=tile, in_=tile, compare_op=ALU.is_ge, fill=0.0, base=0,
                                            pattern=[[0, HG], [1, P]], channel_multiplier=-1).then_inc(tile_masked, 1)
                elif kind == "yo" and i % GB == GB - 1:
                    t = i // GB
                    g = group(t)
                    pool.wait_ge(h_mom, GB * (t + 1))
                    nc.gpsimd.tensor_tensor(ms2[:, g], mom2[:, g, 0], mom2[:, g, 0], ALU.mult).then_inc(h_pool, 1)
                    pool.wait_ge(h_pool, 4 * t + 1)
                    nc.gpsimd.tensor_tensor(ms2[:, g], ms2[:, g], mom2[:, g, 1], ALU.add).then_inc(h_pool, 1)
                    pool.wait_ge(h_pool, 4 * t + 2)
                    nc.gpsimd.tensor_scalar(ms2[:, g], ms2[:, g], EPS, None, ALU.add).then_inc(h_pool, 1)
                    pool.wait_ge(h_pool, 4 * t + 3)
                    nc.gpsimd.tensor_tensor(r2[:, g], ms2[:, g], half_neg[:, g], ALU.pow).then_inc(h_pool, 1)
                    pool.wait_ge(h_pool, 4 * t + 4)
                    for b in range(GB * t, GB * t + GB):
                        nc.gpsimd.tensor_scalar(xn2[:, b, :], hid[:, b, :], r2[:, b:b + 1], None, ALU.mult).then_inc(xn2_ready, 1)
                    nc.gpsimd.tensor_tensor(x1h[:, g, :], X1[:, g, :], hid[:, g, :], ALU.add).then_inc(x1h_ready, 1)
                elif kind == "rt":
                    g = group(i)
                    pool.wait_ge(route, ROUTE_STEPS * (i + 1))
                    if i >= 1:
                        pool.wait_ge(filled, turn["ec", i - 1, 3] + 1)
                    wide = comb_b.rearrange("p b (e n) -> p (b e) n", e=E)
                    narrow = comb[:, g, :].rearrange("p b e -> p (b e)").unsqueeze(2).to_broadcast([P, GB * E, EI])
                    nc.gpsimd.tensor_copy(wide, narrow).then_inc(comb_ready, 1)


_OUT = [((1, 2048, 128), "float32")]


def kernel(**inputs):
    import numpy as _np
    import concourse.bacc as _bacc
    from concourse import mybir as _mybir
    from concourse.bass_utils import run_bass_kernel_spmd as _run

    a = {k: _np.asarray(v) for k, v in inputs.items()}
    wq = a["L0_ffn_Wq"].reshape(P, H, 64)
    wkva = a["L0_ffn_Wkva"]
    pairs_first = _np.concatenate([_np.arange(0, ROPE, 2), _np.arange(1, ROPE, 2)])
    w_all = _np.zeros((P, H + 1, KD), _np.float32)
    w_all[:, :H, LAT:] = wq[:, :, NOPE + pairs_first]
    w_all[:, H, :LAT] = wkva[:, :LAT]
    w_all[:, H, LAT:] = wkva[:, LAT + pairs_first]
    by_quarter = lambda w: w.reshape(4, P, -1).transpose(1, 0, 2)
    w_nope = by_quarter(wq[:, :, :NOPE].transpose(1, 2, 0).reshape(H * NOPE, P))
    w_kv = by_quarter(a["L0_ffn_Wkvb"].T)
    w_out = by_quarter(a["L0_ffn_Wo"].reshape(H, 64, P)[:, :NOPE].reshape(H * NOPE, P))
    with_shared = lambda w, s: _np.concatenate([w, s]).transpose(1, 0, 2)
    freqs = (_np.float32(1.0) / _np.float32(100000.0) ** (_np.arange(0, ROPE, 2, dtype=_np.float32) / _np.float32(ROPE))).astype(_np.float32)
    ang = _np.outer(_np.arange(N, dtype=_np.float32), freqs).astype(_np.float32)
    c, s = _np.cos(ang), _np.sin(ang)
    by_block = lambda t: t.reshape(NB, P, ROPE).transpose(1, 0, 2)
    cos = by_block(_np.concatenate([c, c], 1))
    sin = by_block(_np.concatenate([-s, s], 1))
    column = lambda v: v.reshape(P, 1)
    arrays = {
        "x": a["L0_attn_x"].reshape(N, P),
        "w_spin": a["L0_attn_W_spin"].T, "b_spin": column(a["L0_attn_b_spin"]), "w_global": a["L0_attn_W_global"].T,
        "w_j": a["L0_attn_W_J"].T, "beta": _np.broadcast_to(a["L0_attn_beta"], (P, 1)),
        "w_ln1": column(a["L0_ffn_w_ln1"]), "w_ln2": column(a["L0_ffn_w_ln2"]),
        "w_nope": w_nope, "w_all": w_all, "w_kv": w_kv, "w_out": w_out,
        "w_gate": a["L0_ffn_Wgate"], "e_bias": _np.broadcast_to(a["L0_ffn_expert_bias"], (P, E)),
        "w_eg": with_shared(a["L0_ffn_Wg"], a["L0_ffn_sWg"]), "w_eu": with_shared(a["L0_ffn_Wu"], a["L0_ffn_sWu"]),
        "w_ed": a["L0_ffn_Wd"].reshape(E // 2, P, P).transpose(1, 0, 2), "w_sd": a["L0_ffn_sWd"].reshape(EI, P),
        "ident": _np.eye(P, dtype=_np.float32), "future": _np.triu(_np.full((P, P), -BIG, _np.float32), 1),
        "iota": _np.broadcast_to(_np.arange(E, dtype=_np.float32), (P, E)), "cos": cos, "sin": sin,
    }
    nc = _bacc.Bacc("TRN2", target_bir_lowering=False, num_devices=1)
    maps, args = {}, []
    for name, v in arrays.items():
        v = _np.ascontiguousarray(v)
        maps[f"in_{name}"] = v
        args.append(nc.dram_tensor(f"in_{name}", v.shape, _mybir.dt.from_np(v.dtype), kind="ExternalInput").ap())
    args.append(nc.dram_tensor("out_0", (N, P), _mybir.dt.float32, kind="ExternalOutput").ap())
    build(nc, *args)
    r = _run(nc, [maps], core_ids=[0])
    return r.results[0]["out_0"].reshape(_OUT[0][0])
```

```python
from contextlib import ExitStack

import concourse.bass as bass
from concourse import mybir
from concourse.alu_op_type import AluOpType as ALU

F32 = mybir.dt.float32
F32R = mybir.dt.float32r
U32 = mybir.dt.uint32
ACT = mybir.ActivationFunctionType
AX = mybir.AxisListType

P = 128
N = 2048
NB = N // P
GB = 4
NG = NB // GB
BANK = 512
H = 16
HG = 4
LAT = 16
ROPE = 32
NOPE = 32
KD = LAT + ROPE
VW = 32
EXPERT_BLOCKS = ((0, 4), (4, 4), (8, 4), (12, 3), (15, 1))
E = 8
EI = 64
EPS = 1e-5
BIG = 1e30
SCALE_A = 1.0 / float(P) ** 0.5
SCALE_B = 0.125
SLOTS = 16
AV_LAG = 3
Y_LAG = 2
PREP = 50
X_LAG = 8
ROW_LAG = 2
NM_LEAD = 5
EARLY = 9
ST_BANKS = (0, 1)
MX_BANKS = (2, 4, 5)
SB, MB = len(ST_BANKS), len(MX_BANKS)
LAST_BANKS = ST_BANKS + MX_BANKS
LB = len(LAST_BANKS)


def key_blocks(i):
    return [i] + list(range(i))


NORM_AT = {(3, 3): [("ln", 2)], (3, 7): [("ly", 2)], (8, 24): [("ln", 3)], (8, 31): [("ly", 3)]}

EMPTIES = {"lt": "dve", "xr": "act", "qp": "act", "tq": "act", "tk": "act", "nm": "act", "yt": "dve", "yn": "act", "yo": "dve",
           "hx": "act", "lg": "dve", "eg": "gate", "eu": "dve", "ec": "dve", "ed": "dve"}


def plan_layers():

    def project(i):
        return [("xr", i), ("qp", i, 0), ("qp", i, 1)]

    def stack(i):
        return [("tk", i)] + [("tq", i, g) for g in range(4)]

    def maxima(i):
        return [("mx", i, h, c) for h in range(H) for c in range(i // 4 + 1)]

    def experts(t):
        steps = [("hx", t), ("lg", t), ("eg", t, 0), ("lx", t), ("eu", t, 0), ("ra", t), ("rb", t), ("rt", t), ("eg", t, 1), ("eu", t, 1)]
        steps += [("eg", t, 2), ("eu", t, 2), ("ec", t, 0), ("eg", t, 3), ("eu", t, 3), ("ec", t, 1), ("eg", t, 4), ("eu", t, 4)]
        return steps + [("ec", t, 2), ("ec", t, 3), ("ed", t)]

    early = {}
    for i in range(4):
        for m, step in enumerate(project(i)):
            early[i + 10, m] = step
        for m, step in enumerate(stack(i) if i < 3 else []):
            early[i + 11, m + 4] = step
    first, second = maxima(0), maxima(1)
    plan = []
    for n in range(NB // 2):
        plan += [("lf", n)] + first[2 * n:2 * n + 2]
    plan.append(("nr", 0))
    for n in range(NB // 2):
        plan += [("lf", NB // 2 + n)] + second[2 * n:2 * n + 2]
        if n == 1:
            plan.append(("nm", 0))
    plan += [("nr", 1), ("st", 0, 0, 0), ("nm", 1)]
    late = []
    slot = 0
    side = []
    for i in range(NB):
        tiles = [(g, j) for j in key_blocks(i) for g in range(4)]
        count = len(tiles)
        y_lag = min(Y_LAG, i + 1)
        by = max(count - NM_LEAD, count * 4 // 10) if i > 0 else count
        maxi = maxima(i + 1) if 1 <= i < NB - 1 else []
        if i < 2:
            maxi = maxima(2)[:H // 2] if i == 0 else maxima(2)[H // 2:]
        prep = (stack(i + 2) if 1 <= i < NB - 2 else []) + (project(i + 3) if 1 <= i < NB - 3 else [])
        prep_by = max(1, count * PREP // 100)
        starts = [first for first, _ in EXPERT_BLOCKS]
        if i in starts[1:]:
            t, start = starts.index(i) - 1, slot + AV_LAG + 4 * Y_LAG + X_LAG
            end = slot + 4 * sum(range(i + 1, i + 1 + EXPERT_BLOCKS[t + 1][1])) - 4
            steps = experts(t)
            side = [(start + (end - start) * n // len(steps), step) for n, step in enumerate(steps)]
        for n, (g, j) in enumerate(tiles):
            if slot > 0:
                plan.append(("st", i, g, j))
            if g == 3:
                wait = AV_LAG + (4 if j == i and i > 0 else 0)
                late.append((slot + wait, len(late), ("av", i, j)))
            if n == count - 1:
                for m, kind in enumerate(("yt", "yn", "yo")):
                    late.append((slot + AV_LAG + (m + 1) * y_lag, 99, (kind, i)))
            part = maxi[min(n, by) * len(maxi) // by:min(n + 1, by) * len(maxi) // by]
            plan += part[:len(part) // 2]
            plan += [x[2] for x in sorted(late) if x[0] <= slot]
            late = [x for x in late if x[0] > slot]
            plan += part[len(part) // 2:]
            if n + 1 == by and maxi and i > 0:
                plan.append(("nr", i + 1))
            if n + 1 == min(by + ROW_LAG, count) and maxi and i > 0:
                plan.append(("nm", i + 1))
            plan += prep[min(n, prep_by) * len(prep) // prep_by:min(n + 1, prep_by) * len(prep) // prep_by]
            plan += [step for at, step in side if at == slot]
            if i == 0 and n == 1:
                plan += [("lt",), ("lh",)]
            plan += NORM_AT.get((i, n), [])
            slot += 1
    plan += [x[2] for x in sorted(late)] + experts(len(EXPERT_BLOCKS) - 1)
    spaced, gate, turns = [], None, 0
    for step in plan:
        turns += step[0] in EMPTIES
        if gate and (turns == 2 or step == ("eu",) + gate):
            spaced.append(("gc",) + gate)
            gate = None
        spaced.append(step)
        if gate and step[0] == "st":
            spaced.append(("gc",) + gate)
            gate = None
        if step[0] == "eg":
            gate, turns = step[1:], 0
    return early, spaced


def build(nc, x, w_spin, b_spin, w_global, w_j, beta, w_ln1, w_ln2, w_nope, w_all, w_kv, w_out,
          w_gate, e_bias, w_eg, w_eu, w_ed, w_sd, ident, future, iota, cos, sin, out):
    early, plan = plan_layers()
    turn, emptied, tally = {}, [], {"act": 0, "dve": 0, "gate": 0}
    all_steps = [early[at] for at in sorted(early)] + plan
    max_no, tile_no, av_no = {}, {}, {}
    for step in all_steps:
        if step[0] in EMPTIES:
            who = EMPTIES[step[0]]
            tally[who] += 1
            turn[step] = len(emptied)
            emptied.append((who, tally[who]))
        elif step[0] == "mx":
            max_no[step] = len(max_no)
        elif step[0] == "st":
            tile_no[step[1:]] = len(tile_no)
        elif step[0] == "av":
            av_no[step] = len(av_no)
    av_order = {}
    for _, i, j in av_no:
        av_order.setdefault(i, []).append(j)
    tile_keys = {n: key for key, n in tile_no.items()}

    def av_count(n):
        i, _, j = tile_keys[n]
        return av_no["av", i, j] + 1

    last_tiles = tile_no[NB - 1, 0, NB - 1]

    def tile_bank(n):
        return ST_BANKS[n % SB] if n < last_tiles else LAST_BANKS[(n - last_tiles) % LB]

    assert last_tiles % SB == 0

    def chunk(i, c):
        k0, k1 = c * BANK, min((c + 1) * BANK, (i + 1) * P)
        return k0, k1, (i * P - k0 if k1 == (i + 1) * P else k1 - k0)

    ctx = ExitStack()
    with ctx:
        def sb(name, shape, dt=F32):
            return ctx.enter_context(nc.sbuf_tensor(name, shape, dt))

        def sem(name):
            return ctx.enter_context(nc.semaphore(name))

        psum = ctx.enter_context(nc.psum_tensor("psum", [P, 8, BANK], F32))

        wsp = sb("wsp", [P, P]); wgl = sb("wgl", [P, P]); wj = sb("wj", [P, P])
        bsp = sb("bsp", [P, 1]); bet = sb("bet", [P, 1]); ln1 = sb("ln1", [P, 1]); ln2 = sb("ln2", [P, 1])
        wall = sb("wall", [P, H + 1, KD]); wkv = sb("wkv", [P, 4, LAT])
        wgate = sb("wgate", [P, E]); ebias = sb("ebias", [P, E])
        weg = sb("weg", [P, E + 1, EI]); weu = sb("weu", [P, E + 1, EI])
        wed = sb("wed", [P, E // 2, P]); wsd = sb("wsd", [EI, P])
        idn = sb("idn", [P, P]); fut = sb("fut", [P, P]); iot = sb("iot", [P, E])
        cs = sb("cs", [P, NB, ROPE]); sn = sb("sn", [P, NB, ROPE])
        idr = sb("idr", [P, P], F32R)
        half_neg = sb("half_neg", [P, NB])
        staging = sb("staging", [P, 2 * P + (H + 1) * (KD + ROPE)])
        wnope = staging[:, 0:4 * P].rearrange("p (k c) -> p k c", k=4)
        wout = staging[:, 4 * P:8 * P].rearrange("p (k c) -> p k c", k=4)
        kv_diag = staging[:, 8 * P:8 * P + 4 * HG * LAT].rearrange("p (k c) -> p k c", k=4)
        xrT = staging[:, 0:2 * P].rearrange("p (a n) -> p a n", a=2)
        raw = staging[:, 2 * P:2 * P + (H + 1) * KD].rearrange("p (h d) -> p h d", d=KD)
        rot = staging[:, 2 * P + (H + 1) * KD:].rearrange("p (h d) -> p h d", d=ROPE)
        wvo = sb("wvo", [P, 2, P])

        X = sb("X", [P, NB, P]); X1 = X; Y = sb("Y", [P, NB, P]); YR = sb("YR", [P, NB, P])
        stats = sb("stats", [P, NB, 6]); mom = sb("mom", [P, NB, 2]); var_e = sb("var_e", [P, NB]); rstd = sb("rstd", [P, NB])
        xn = YR
        xnT = sb("xnT", [P, N]); s_high = sb("s_high", [P, N], F32R); s_tok = sb("s_tok", [P, NB, P]); sg = Y
        mean_parts = sb("mean_parts", [P, NG]); mean_sum = sb("mean_sum", [P, 1]); mean_b = sb("mean_b", [P, P]); gi = sb("gi", [P, P])
        region = sb("region", [P, 2 * N + 2 * NB * BANK])
        prob = region[:, 0:2 * N].rearrange("p (a n) -> p a n", a=2)
        sT = prob[:, 1, :]
        probT = region[:, 2 * N:2 * N + 2 * NB * BANK].rearrange("p (a m n) -> p a m n", a=2, m=NB)
        hmax = sb("hmax", [P, NB, 2]); rsum2 = sb("rsum2", [P, NB, 2]); nbias = sb("nbias", [P, NB]); rsum = sb("rsum", [P, NB]); rden = sb("rden", [P, NB])
        oT = xnT[:, 2 * BANK:3 * BANK]; z = xnT[:, 3 * BANK:4 * BANK]
        th = z
        stats1 = sb("stats1", [P, NB, 6]); mom1 = sb("mom1", [P, NB, 2])
        ve1 = sb("ve1", [P, NB]); rs1 = sb("rs1", [P, NB]); sq1 = sb("sq1", [P, NB]); ms1 = sb("ms1", [P, NB]); me1 = sb("me1", [P, NB]); rr1 = sb("rr1", [P, NB])

        qT = sb("qT", [P, 3, H * P], F32R)
        kT = sb("kT", [P, 2, N], F32R)
        wj_high, wj_low = qT[:, 2, 2 * BANK:2 * BANK + P], qT[:, 2, 2 * BANK + P:2 * BANK + 2 * P]
        e_high = [qT[:, 2, 0:BANK], kT[:, 0, BANK:2 * BANK]]
        e_low = [qT[:, 2, BANK:2 * BANK], kT[:, 0, 2 * BANK:3 * BANK]]
        s_low0 = sb("s_low0", [P, BANK], F32R)
        s_low = [s_low0[:, :]] + [kT[:, 1, t * BANK:(t + 1) * BANK] for t in range(1, NG)]
        used = 0

        def take(count):
            nonlocal used
            used += count
            return region[:, used - count:used]

        val = sb("val", [P, NB, VW])
        pb = take(SLOTS * BANK).rearrange("p (s n) -> p s n", s=SLOTS)
        qs = sb("qs", [P, H + 1, 2, KD], F32R)
        ks = sb("ks", [P, 2, 2, KD], F32R)
        part_max = take(2 * H * 5).rearrange("p (a h c) -> p a h c", a=2, h=H)
        masked = [mean_b, gi]
        neg_max = take(H)
        acc_s = take(BANK)
        yden = take(H).rearrange("p (m g) -> p m g", m=HG)
        ynorm = take(H * LAT).rearrange("p (h d) -> p h d", h=H)
        yT = take(2 * P).rearrange("p (a n) -> p a n", a=2)
        neg_maxT = sb("neg_maxT", [H, P], F32R)
        hid = xnT[:, :].rearrange("p (b c) -> p b c", b=NB)
        stats2 = stats; mom2 = mom
        ms2 = take(NB); r2 = take(NB)
        xn2 = YR
        x1h = s_tok
        logit = take(NB * E).rearrange("p (b e) -> p b e", b=NB)
        lmax = take(NB)
        lshift = take(NB * E).rearrange("p (b e) -> p b e", b=NB)
        pe_ = take(NB * E).rearrange("p (b e) -> p b e", b=NB)
        top = take(NB * E).rearrange("p (b e) -> p b e", b=NB)
        idx = take(NB * E).bitcast(U32).rearrange("p (b e) -> p b e", b=NB)
        idxf = take(NB * 2).rearrange("p (b e) -> p b e", b=NB)
        pick0 = take(NB * E).rearrange("p (b e) -> p b e", b=NB)
        pick1 = take(NB * E).rearrange("p (b e) -> p b e", b=NB)
        pick = take(NB * E).rearrange("p (b e) -> p b e", b=NB)
        chosen = take(NB * E).rearrange("p (b e) -> p b e", b=NB)
        csum = take(NB)
        crec = take(NB)
        comb = take(NB * E).rearrange("p (b e) -> p b e", b=NB)
        tg = take(BANK); gs = take(BANK); ga = take(BANK)
        hT = take(5 * BANK).rearrange("p (k n) -> p k n", k=5)
        comb_b = take(GB * E * EI).rearrange("p (b n) -> p b n", b=GB)
        res = take(BANK)
        xfT = take(BANK)

        x_in = [sem(f"x_in{t}") for t in range(NG)]; idn_in = sem("idn_in"); w_in = sem("w_in"); w2_in = sem("w2_in")
        const_set = sem("const_set"); k_one_set = sem("k_one_set"); kv_zero = sem("kv_zero"); kv_placed = sem("kv_placed")
        idr_ready = sem("idr_ready"); sd_half = sem("sd_half")
        absorb_filled = sem("absorb_filled"); absorb_ready = sem("absorb_ready")
        x_stats = sem("x_stats"); x_mom = sem("x_mom"); x_var = sem("x_var"); x_rstd = sem("x_rstd"); xn_ready = sem("xn_ready")
        xnT_filled = sem("xnT_filled"); xnT_ready = sem("xnT_ready")
        s_filled = sem("s_filled"); s_ready = sem("s_ready"); st_filled = sem("st_filled"); st_ready = sem("st_ready")
        mean_step = sem("mean_step"); gi_filled = sem("gi_filled"); gi_ready = sem("gi_ready"); sg_ready = sem("sg_ready")
        e_filled = sem("e_filled"); e_ready = sem("e_ready"); e_low_ready = sem("e_low_ready"); s_low_ready = sem("s_low_ready"); wj_split = sem("wj_split")
        sc_filled = sem("sc_filled"); max_found = sem("max_found"); bias_ready = sem("bias_ready"); exp_done = sem("exp_done")
        pT_filled = sem("pT_filled"); pT_ready = sem("pT_ready")
        o_filled = sem("o_filled"); oT_ready = sem("oT_ready"); ot_filled = sem("ot_filled")
        rden_ready = sem("rden_ready"); z_ready = sem("z_ready"); th_ready = sem("th_ready"); x1_ready = sem("x1_ready")
        y_stats = sem("y_stats"); y_mom = sem("y_mom"); y_pool = sem("y_pool"); y_rms = sem("y_rms"); y_ready = sem("y_ready"); yr_ready = sem("yr_ready")
        filled = sem("filled"); act_emptied = sem("act_emptied"); dve_emptied = sem("dve_emptied")
        rotated = sem("rotated"); q_high = sem("q_high"); q_split = sem("q_split")
        tile_filled = sem("tile_filled"); tile_exp = sem("tile_exp"); tile_masked = sem("tile_masked"); av_done = sem("av_done")
        acc_emptied = sem("acc_emptied")
        max_filled = sem("max_filled"); max_emptied = sem("max_emptied"); neg_max_ready = sem("neg_max_ready"); max_row_in = sem("max_row_in")
        yden_ready = sem("yden_ready")
        h_stats = sem("h_stats"); h_mom = sem("h_mom"); h_pool = sem("h_pool"); xn2_ready = sem("xn2_ready"); x1h_ready = sem("x1h_ready")
        route = sem("route"); comb_ready = sem("comb_ready"); lexp_ready = sem("lexp_ready")
        gate_copied = sem("gate_copied"); ga_done = sem("ga_done")
        out_done = [sem(f"out_done{t}") for t in range(len(EXPERT_BLOCKS))]

        block = ctx.enter_context(nc.Block())

        x_view = x.rearrange("(b p) c -> p b c", p=P)
        out_view = out.rearrange("(b p) c -> p b c", p=P)
        first_loads = [(wsp, w_spin), (bsp, b_spin), (wgl, w_global), (wj, w_j), (bet, beta)]
        later_loads = [(ln1, w_ln1), (ln2, w_ln2), (wnope, w_nope), (wall, w_all), (wkv, w_kv), (wout, w_out),
                       (wgate, w_gate), (ebias, e_bias), (weg, w_eg), (weu, w_eu), (wed, w_ed), (wsd, w_sd),
                       (fut, future), (iot, iota), (cs, cos), (sn, sin)]
        W1 = 16 * len(first_loads)
        W2 = 16 * len(later_loads)

        def tokens(t):
            return slice(t * BANK, (t + 1) * BANK)

        def group(t):
            return slice(t * GB, (t + 1) * GB)

        def expert_blocks(t):
            first, count = EXPERT_BLOCKS[t]
            return slice(first, first + count)

        def bank4(b):
            return psum[:, b, :].rearrange("p (a c) -> p a c", a=GB)

        def misc(T):
            return psum[:, 7 if T < len(early) else 6 + (T - len(early)) % 2, :]

        def turn_before(T):
            E0 = len(early)
            return T - 1 if 0 < T < E0 else T - 2 if T >= E0 + 2 else None

        def wait_emptied(eng, T):
            who, count = emptied[T]
            eng.wait_ge({"act": act_emptied, "dve": dve_emptied, "gate": gate_copied}[who], count)

        HALVES = ((0, 1 + H // 2), (1 + H // 2, 1 + H))
        ROUTE_STEPS = 12

        @block.sync
        def _(sp):
            for t in range(NG):
                sp.dma_start(X[:, group(t), :], x_view[:, group(t), :]).then_inc(x_in[t], 16)
                if t == 0:
                    sp.dma_start(idn[:], ident).then_inc(idn_in, 16)
            for dst, src in first_loads:
                sp.dma_start(dst[:], src).then_inc(w_in, 16)
            for dst, src in later_loads:
                sp.dma_start(dst[:], src).then_inc(w2_in, 16)
            for step in plan:
                if step[0] == "nm":
                    i = step[1]
                    wait_emptied(sp, turn[step])
                    sp.dma_start(qT[2 * KD:2 * KD + 1, i % 3, :].bitcast(F32), neg_maxT[:, :].bitcast(F32)).then_inc(max_row_in, 16)
                elif step[0] == "ed":
                    t = step[1]
                    wait_emptied(sp, turn[step])
                    count = EXPERT_BLOCKS[t][1]
                    sp.dma_start(out_view[:, expert_blocks(t), :], res[:, 0:count * P].rearrange("p (b c) -> p b c", b=count)).then_inc(out_done[t], 16)
            for t in range(len(EXPERT_BLOCKS)):
                sp.wait_ge(out_done[t], 16)

        @block.tensor
        def _(pe):
            def transpose(dst, src):
                rows = src.shape[0]
                return nc.tensor.transpose(dst, src, idn[0:rows, 0:rows])

            pe.wait_ge(idn_in, 16)
            for t in range(NG):
                pe.wait_ge(xn_ready, GB * (t + 1))
                if t >= 2:
                    pe.wait_ge(xnT_ready, t - 1)
                for u in range(GB):
                    last = transpose(psum[:, 4 + t % 2, u * P:(u + 1) * P], xn[:, GB * t + u, :])
                last.then_inc(xnT_filled, 1)
            pe.wait_ge(w_in, W1)
            for t in range(NG):
                pe.wait_ge(xnT_ready, t + 1)
                if t >= 2:
                    pe.wait_ge(s_ready, t - 1)
                nc.tensor.matmul(psum[:, 6 + t % 2, :], wsp[:], xnT[:, tokens(t)], start=True, stop=True).then_inc(s_filled, 1)

            def spins_by_tokens(t):
                pe.wait_ge(s_ready, t + 1)
                if t < 2:
                    pe.wait_ge(xnT_ready, NG)
                else:
                    pe.wait_ge(st_ready, t - 1)
                for u in range(GB):
                    last = transpose(psum[:, 4 + t % 2, u * P:(u + 1) * P], sT[:, (GB * t + u) * P:(GB * t + u + 1) * P])
                last.then_inc(st_filled, 1)

            def absorb():
                pe.wait_ge(w2_in, W2)
                pe.wait_ge(kv_placed, 16)
                for k in range(4):
                    last = nc.tensor.matmul(psum[:, 6, k * 64:(k + 1) * 64], wnope[:, k, :], kv_diag[:, k, :], start=True, stop=True)
                last.then_inc(absorb_filled, 1)
                for k in range(4):
                    c = BANK // 2 + (k // 2) * P
                    last = nc.tensor.matmul(psum[64 * (k % 2):64 * (k % 2) + 64, 6, c:c + P], kv_diag[:, k, :],
                                            wout[:, k, :], start=True, stop=True)
                last.then_inc(absorb_filled, 1)

            def global_field():
                pe.wait_ge(mean_step, 3)
                pe.wait_ge(absorb_ready, 2)
                nc.tensor.matmul(psum[:, 6, 0:P], mean_b[:], wgl[:], start=True, stop=True).then_inc(gi_filled, 1)

            def energy(t):
                pe.wait_ge(s_ready, NG)
                pe.wait_ge(s_low_ready, t + 1)
                pe.wait_ge(wj_split, 2)
                if t >= 1:
                    pe.wait_ge(e_low_ready, t)
                nc.tensor.matmul(psum[:, 7, :], wj_high, s_high[:, tokens(t)], start=True, stop=False)
                nc.tensor.matmul(psum[:, 7, :], wj_high, s_low[t], start=False, stop=False)
                nc.tensor.matmul(psum[:, 7, :], wj_low, s_high[:, tokens(t)], start=False, stop=True).then_inc(e_filled, 1)

            def probs_transposed(n, k):
                pe.wait_ge(exp_done, 2 * n + 1 + k // 2)
                if 4 * n + k >= 2:
                    pe.wait_ge(pT_ready, 4 * n + k - 1)
                for m in range(4):
                    last = transpose(psum[:, 4 + k % 2, m * P:(m + 1) * P], prob[:, n % 2, (4 * k + m) * P:(4 * k + m + 1) * P])
                last.then_inc(pT_filled, 1)

            def local_field(t, m0, m1):
                pe.wait_ge(pT_ready, 16 * (t + 1))
                if t == 0 and m0 == 0:
                    pe.wait_ge(gi_ready, 1)
                if 1 <= t < NG - 1 and m0 == 0:
                    pe.wait_ge(z_ready, GB * t)
                for m in range(m0, m1):
                    last = nc.tensor.matmul(psum[:, 6 if t < NG - 1 else 3, :], s_tok[:, m, :], probT[:, t % 2, m, :],
                                            start=(m == 0), stop=(m == NB - 1))
                if m1 == NB:
                    last.then_inc(o_filled, 1)

            def local_field_by_tokens(t, dst):
                pe.wait_ge(oT_ready, t + 1)
                for u in range(GB):
                    last = transpose(dst[:, u * P:(u + 1) * P], oT[:, u * P:(u + 1) * P])
                last.then_inc(ot_filled if t < NG - 1 else filled, 1)

            def follow(step):
                kind, i = step[0], step[1] if len(step) > 1 else None
                T = turn.get(step)
                if T is not None and turn_before(T) is not None:
                    wait_emptied(pe, turn_before(T))
                if kind == "lf":
                    local_field(NG - 1, i, i + 1)
                elif kind == "lt":
                    local_field_by_tokens(NG - 1, misc(T))
                elif kind == "xr":
                    pe.wait_ge(yr_ready, i + 1)
                    transpose(misc(T)[:, 0:P], YR[:, i, :]).then_inc(filled, 1)
                elif kind == "qp":
                    h0, h1 = HALVES[step[2]]
                    wait_emptied(pe, turn["xr", i])
                    nc.tensor.matmul(misc(T)[:, 0:(h1 - h0) * KD], xrT[:, i % 2, :], wall[:, h0:h1, :], start=True, stop=True).then_inc(filled, 1)
                elif kind == "tk":
                    pe.wait_ge(q_split, i + 1)
                    for c in range(2):
                        last = nc.tensor.matmul(misc(T)[0:2 * KD, c * P:(c + 1) * P], ks[:, c, :, :], idr[:], start=True, stop=True)
                    last.then_inc(filled, 1)
                elif kind == "tq":
                    g = step[2]
                    if g == 2:
                        pe.wait_ge(q_high, 4 * i + 4)
                    for m in range(HG):
                        last = nc.tensor.matmul(misc(T)[0:2 * KD, m * P:(m + 1) * P], qs[:, 1 + HG * g + m, :, :], idr[:], start=True, stop=True)
                    last.then_inc(filled, 1)
                elif kind == "mx":
                    _, _, h, c = step
                    m = max_no[step]
                    if m >= MB:
                        pe.wait_ge(max_emptied, m - MB + 1)
                    wait_emptied(pe, turn["tq", i, h // HG])
                    k0, k1, _ = chunk(i, c)
                    last = nc.tensor.matmul(psum[:, MX_BANKS[m % MB], 0:k1 - k0], qT[0:2 * KD, i % 3, h * P:(h + 1) * P],
                                            kT[0:2 * KD, 0, k0:k1], start=True, stop=True)
                    last.then_inc(max_filled, 1)
                elif kind == "nm":
                    pe.wait_ge(neg_max_ready, i + 1)
                    transpose(misc(T)[0:H, 0:P], neg_max[:, :]).then_inc(filled, 1)
                elif kind == "st":
                    _, _, g, j = step
                    n = tile_no[i, g, j]
                    if g == 0 and j == i:
                        pe.wait_ge(max_row_in, 16 * (i + 1))
                    if n - last_tiles >= LB:
                        pe.wait_ge(tile_exp, n - LB + 1)
                    elif n - last_tiles >= SB:
                        pe.wait_ge(max_emptied, len(max_no))
                    elif n >= SB:
                        pe.wait_ge(tile_exp, n - SB + 1)
                    cols = slice(g * BANK, (g + 1) * BANK)
                    nc.tensor.matmul(psum[:, tile_bank(n), :], kT[0:2 * KD + 1, 0, j * P:(j + 1) * P], qT[0:2 * KD + 1, i % 3, cols],
                                     start=True, stop=False)
                    nc.tensor.matmul(psum[:, tile_bank(n), :], kT[0:2 * KD, 1, j * P:(j + 1) * P], qT[0:2 * KD, i % 3, cols],
                                     start=False, stop=True).then_inc(tile_filled, 1)
                elif kind == "av":
                    j = step[2]
                    first, final = j == av_order[i][0], j == av_order[i][-1]
                    if first:
                        pe.wait_ge(acc_emptied, i) if i >= 1 else pe.wait_ge(oT_ready, NG)
                    pe.wait_ge(tile_exp, tile_no[i, 3, j] + 1)
                    if j == i:
                        pe.wait_ge(tile_masked, 4 * (i + 1))
                    for g in range(4):
                        last = nc.tensor.matmul(psum[VW * g:VW * (g + 1), 3, :], val[:, j, :], pb[:, tile_no[i, g, j] % SLOTS, :],
                                                start=first, stop=final)
                    last.then_inc(av_done, 1)
                elif kind == "yt":
                    pe.wait_ge(acc_emptied, i + 1)
                    for m in range(HG):
                        last = transpose(misc(T)[:, m * P:(m + 1) * P], acc_s[:, m * P:(m + 1) * P])
                    last.then_inc(filled, 1)
                elif kind == "yn":
                    wait_emptied(pe, turn["yt", i])
                    for k in range(2):
                        last = transpose(misc(T)[:, k * P:(k + 1) * P], ynorm[:, 8 * k:8 * k + 8, :])
                    last.then_inc(filled, 1)
                elif kind == "yo":
                    wait_emptied(pe, turn["yn", i])
                    for k in range(2):
                        last = nc.tensor.matmul(misc(T)[:, 0:P], yT[:, k, :], wvo[:, k, :], start=(k == 0), stop=(k == 1))
                    last.then_inc(filled, 1)

                elif kind == "hx":
                    first, count = EXPERT_BLOCKS[i]
                    pe.wait_ge(xn2_ready, first + count)
                    for u in range(count):
                        last = transpose(misc(T)[:, u * P:(u + 1) * P], xn2[:, first + u, :])
                    last.then_inc(filled, 1)
                elif kind == "lg":
                    first, count = EXPERT_BLOCKS[i]
                    wait_emptied(pe, turn["hx", i])
                    for u in range(count):
                        last = nc.tensor.matmul(misc(T)[:, u * E:(u + 1) * E], xfT[:, u * P:(u + 1) * P], wgate[:], start=True, stop=True)
                    last.then_inc(filled, 1)
                elif kind in ("eg", "eu"):
                    k, width = step[2], EXPERT_BLOCKS[i][1] * P
                    rows, es = (P, slice(2 * k, 2 * k + 2)) if k < 4 else (EI, slice(E, E + 1))
                    nc.tensor.matmul(misc(T)[0:rows, 0:width], (weg if kind == "eg" else weu)[:, es, :], xfT[:, 0:width],
                                     start=True, stop=True).then_inc(filled, 1)
                elif kind == "ec":
                    k = step[2]
                    pe.wait_ge(comb_ready, i + 1)
                    for u in range(EXPERT_BLOCKS[i][1]):
                        last = transpose(misc(T)[:, u * P:(u + 1) * P], comb_b[:, u, 2 * k * EI:(2 * k + 2) * EI])
                    last.then_inc(filled, 1)
                elif kind == "ed":
                    wait_emptied(pe, turn["ec", i, 3])
                    pe.wait_ge(sd_half, 2)
                    for u in range(EXPERT_BLOCKS[i][1]):
                        for k in range(5):
                            rows = P if k < 4 else EI
                            last = nc.tensor.matmul(misc(T)[:, u * P:(u + 1) * P], hT[0:rows, k, u * P:(u + 1) * P],
                                                    wed[:, k, :] if k < 4 else wsd[:], start=(k == 0), stop=(k == 4))
                    last.then_inc(filled, 1)

            energy(0)
            spins_by_tokens(0)
            spins_by_tokens(1)
            for t in range(NG):
                for u in range(GB):
                    n = GB * t + u
                    pe.wait_ge(e_low_ready, t + 1)
                    for half in range(2):
                        if n >= 1:
                            pe.wait_ge(exp_done, 2 * n - 1 + half)
                        for c in (2 * half, 2 * half + 1):
                            if n == 0:
                                pe.wait_ge(s_low_ready, c + 1)
                            high, low = e_high[t % 2][:, u * P:(u + 1) * P], e_low[t % 2][:, u * P:(u + 1) * P]
                            nc.tensor.matmul(psum[:, c, :], high, s_high[:, tokens(c)], start=True, stop=False)
                            nc.tensor.matmul(psum[:, c, :], high, s_low[c], start=False, stop=False)
                            last = nc.tensor.matmul(psum[:, c, :], low, s_high[:, tokens(c)], start=False, stop=True)
                        last.then_inc(sc_filled, 1)
                    if n == 0:
                        spins_by_tokens(2)
                        spins_by_tokens(3)
                        absorb()
                        pe.wait_ge(st_ready, NG)
                        pe.wait_ge(idr_ready, 1)
                    if n == 1:
                        global_field()
                    if u == 1 and t < NG - 1:
                        energy(t + 1)
                    if t >= 2 and u == 0:
                        local_field_by_tokens(t - 2, psum[:, 6, :])
                    for m in range(EARLY):
                        if m < 4 and n >= 1:
                            probs_transposed(n - 1, m)
                        if 4 <= m < 8 and t >= 1:
                            local_field(t - 1, 4 * u + m - 4, 4 * u + m - 3)
                        if (n, m) in early:
                            pe.wait_ge(e_low_ready, NG)
                            follow(early[n, m])
            for k in range(4):
                probs_transposed(NB - 1, k)
                if k == 1:
                    local_field_by_tokens(NG - 2, psum[:, 6, :])
            pe.wait_ge(exp_done, 2 * NB)
            pe.wait_ge(pT_ready, 4 * NB)
            pe.wait_ge(oT_ready, NG - 1)
            pe.wait_ge(z_ready, GB * (NG - 1))
            pe.wait_ge(const_set, 3)
            pe.wait_ge(k_one_set, 2)

            for step in plan:
                follow(step)

        @block.scalar
        def _(act):
            act.wait_ge(w_in, W1)
            for t in range(NG):
                act.wait_ge(xnT_filled, t + 1)
                nc.scalar.copy(xnT[:, tokens(t)], psum[:, 4 + t % 2, :]).then_inc(xnT_ready, 1)
            for t in range(NG):
                act.wait_ge(s_filled, t + 1)
                nc.scalar.activation(sT[:, tokens(t)], psum[:, 6 + t % 2, :], ACT.Identity, bias=bsp[:], accum_out=mean_parts[:, t:t + 1])
                nc.scalar.activation(s_high[:, tokens(t)], psum[:, 6 + t % 2, :], ACT.Identity, bias=bsp[:]).then_inc(s_ready, 1)

            def absorb():
                act.wait_ge(w2_in, W2)
                act.wait_ge(absorb_filled, 2)
                nc.scalar.copy(wall[:, 1:H + 1, 0:LAT], psum[:, 6, 0:H * LAT].rearrange("p (h r) -> p h r", h=H)).then_inc(absorb_ready, 1)
                nc.scalar.copy(wvo[:], psum[:, 6, BANK // 2:BANK].rearrange("p (k c) -> p k c", k=2)).then_inc(absorb_ready, 1)

            def energy(t):
                act.wait_ge(e_filled, t + 1)
                nc.scalar.mul(e_high[t % 2], psum[:, 7, :], SCALE_A).then_inc(e_ready, 1)

            def probs_transposed(n, k):
                t, u = n // GB, n % GB
                if u == 0 and k == 0 and t >= 2:
                    act.wait_ge(o_filled, t - 1)
                act.wait_ge(pT_filled, 4 * n + k + 1)
                nc.scalar.copy(probT[:, t % 2, 4 * k:4 * k + 4, u * P:(u + 1) * P], bank4(4 + k % 2)).then_inc(pT_ready, 1)

            def field_tanh(t):
                wait_emptied(act, turn["lt",]) if t == NG - 1 else act.wait_ge(z_ready, GB * (t + 1))
                nc.scalar.activation(th[:], z[:], ACT.Tanh, scale=bet[:]).then_inc(th_ready, 1)

            def follow(step):
                kind, i = step[0], step[1] if len(step) > 1 else None
                T = turn.get(step)
                if T is not None and emptied[T][0] in ("act", "gate"):
                    act.wait_ge(filled, T + 1)
                if kind == "lh":
                    field_tanh(NG - 1)
                elif kind == "xr":
                    nc.scalar.activation(xrT[:, i % 2, :], misc(T)[:, 0:P], ACT.Copy, scale=ln1[:]).then_inc(act_emptied, 1)
                elif kind == "qp":
                    h0, h1 = HALVES[step[2]]
                    if i >= 1:
                        act.wait_ge(q_high, 4 * (i - 1) + 2 * step[2] + 2)
                    nc.scalar.copy(raw[:, h0:h1, :], misc(T)[:, 0:(h1 - h0) * KD].rearrange("p (h d) -> p h d", d=KD)).then_inc(act_emptied, 1)
                elif kind == "tk":
                    nc.scalar.copy(kT[0:2 * KD, 0, i * P:(i + 1) * P], misc(T)[0:2 * KD, 0:P])
                    nc.scalar.copy(kT[0:2 * KD, 1, i * P:(i + 1) * P], misc(T)[0:2 * KD, P:2 * P]).then_inc(act_emptied, 1)
                elif kind == "tq":
                    g = step[2]
                    nc.scalar.copy(qT[0:2 * KD, i % 3, g * BANK:(g + 1) * BANK], misc(T)[0:2 * KD, :]).then_inc(act_emptied, 1)
                elif kind == "nm":
                    if i >= 1:
                        act.wait_ge(max_row_in, 16 * i)
                    nc.scalar.copy(neg_maxT[:, :], misc(T)[0:H, 0:P]).then_inc(act_emptied, 1)
                elif kind == "st":
                    n = tile_no[step[1:]]
                    act.wait_ge(tile_filled, n + 1)
                    if n >= SLOTS:
                        act.wait_ge(av_done, av_count(n - SLOTS))
                    nc.scalar.activation(pb[:, n % SLOTS, :], psum[:, tile_bank(n), :], ACT.Exp, scale=SCALE_B).then_inc(tile_exp, 1)
                elif kind == "av" and step[2] == av_order[i][-1]:
                    act.wait_ge(av_done, av_no[step] + 1)
                    if i >= 1:
                        act.wait_ge(filled, turn["yt", i - 1] + 1)
                    nc.scalar.copy(acc_s, psum[:, 3, :]).then_inc(acc_emptied, 1)
                elif kind == "yn":
                    nc.scalar.copy(yT[:], misc(T)[:, 0:2 * P].rearrange("p (k c) -> p k c", k=2)).then_inc(act_emptied, 1)

                elif kind == "hx":
                    if i >= 1:
                        act.wait_ge(filled, turn["eu", i - 1, 4] + 1)
                    nc.scalar.activation(xfT[:, 0:EXPERT_BLOCKS[i][1] * P], misc(T)[:, 0:EXPERT_BLOCKS[i][1] * P], ACT.Copy, scale=ln2[:]).then_inc(act_emptied, 1)
                elif kind == "lx":
                    g = expert_blocks(i)
                    act.wait_ge(route, ROUTE_STEPS * i + 2)
                    nc.scalar.activation(pe_[:, g, :], lshift[:, g, :], ACT.Exp).then_inc(lexp_ready, 1)
                elif kind == "eg":
                    rows, width = P if step[2] < 4 else EI, EXPERT_BLOCKS[i][1] * P
                    if 5 * i + step[2] >= 1:
                        act.wait_ge(ga_done, 5 * i + step[2])
                    nc.scalar.activation(tg[0:rows, 0:width], misc(T)[0:rows, 0:width], ACT.Tanh, scale=0.5)
                elif kind == "gc":
                    rows, width = P if step[2] < 4 else EI, EXPERT_BLOCKS[i][1] * P
                    nc.scalar.copy(gs[0:rows, 0:width], misc(turn["eg", i, step[2]])[0:rows, 0:width]).then_inc(gate_copied, 1)

            energy(0)
            for t in range(NG):
                act.wait_ge(st_filled, t + 1)
                nc.scalar.copy(s_tok[:, group(t), :], bank4(4 + t % 2)).then_inc(st_ready, 1)
            for t in range(NG):
                for u in range(GB):
                    n = GB * t + u
                    if u == 1 and t < NG - 1:
                        energy(t + 1)
                    for m in range(EARLY):
                        if m < 4 and n >= 1:
                            probs_transposed(n - 1, m)
                        if m == 5:
                            act.wait_ge(bias_ready, n + 1)
                        if m in (5, 7):
                            half = (m - 5) // 2
                            nc.scalar.activation(prob[:, n % 2, half * N // 2:(half + 1) * N // 2], psum[:, 2 * half:2 * half + 2, :], ACT.Exp,
                                                 bias=nbias[:, n:n + 1], accum_out=rsum2[:, n, half:half + 1]).then_inc(exp_done, 1)
                        if (n, m) in early:
                            follow(early[n, m])
                    if n == 0:
                        absorb()
                    if t >= 2 and u == 0:
                        field_tanh(t - 2)
            for k in range(4):
                probs_transposed(NB - 1, k)
            field_tanh(NG - 2)

            for step in plan:
                follow(step)

        @block.vector
        def _(dve):
            nc.vector.memset(kT[2 * KD:2 * KD + 1, 0, 0:BANK].bitcast(F32), 1.0)
            nc.vector.memset(kT[2 * KD:2 * KD + 1, 0, 3 * BANK:N].bitcast(F32), 1.0).then_inc(k_one_set, 1)
            for t in range(NG + 1):
                if t < NG:
                    dve.wait_ge(x_in[t], 16)
                    for b in range(GB * t, GB * t + GB):
                        nc.vector.bn_stats(stats[:, b, :], X[:, b, :]).then_inc(x_stats, 1)
                    for b in range(GB * t, GB * t + GB):
                        dve.wait_ge(x_stats, b + 1)
                        nc.vector.bn_aggr(mom[:, b, :], stats[:, b, :]).then_inc(x_mom, 1)
                if t >= 1:
                    dve.wait_ge(x_rstd, t)
                    dve.wait_ge(x_mom, GB * t)
                    for b in range(GB * t - GB, GB * t):
                        nc.vector.tensor_scalar(xn[:, b, :], X[:, b, :], mom[:, b, 0:1], rstd[:, b:b + 1], ALU.subtract, ALU.mult).then_inc(xn_ready, 1)
            dve.wait_ge(w2_in, W2)
            dve.wait_ge(kv_zero, 1)
            for k in range(4):
                for m in range(HG):
                    nc.vector.tensor_copy(kv_diag[NOPE * m:NOPE * m + NOPE, k, LAT * m:LAT * m + LAT],
                                          wkv[NOPE * m:NOPE * m + NOPE, k, :]).then_inc(kv_placed, 1)
            dve.wait_ge(w_in, W1)
            nc.vector.tensor_copy(idr[:], idn[:]).then_inc(idr_ready, 1)
            nc.vector.tensor_scalar(wed[:], wed[:], 0.5, None, ALU.mult).then_inc(sd_half, 1)
            nc.vector.tensor_scalar(wsd[:], wsd[:], 0.5, None, ALU.mult).then_inc(sd_half, 1)
            dve.wait_ge(w_in, W1)
            nc.vector.tensor_copy(wj_high, wj[:]).then_inc(wj_split, 1)
            dve.wait_ge(wj_split, 1)
            nc.vector.tensor_tensor(wj_low, wj[:], wj_high.bitcast(F32), ALU.subtract).then_inc(wj_split, 1)
            for t in range(NG):
                dve.wait_ge(s_ready, t + 1)
                nc.vector.tensor_tensor(s_low[t], sT[:, tokens(t)], s_high[:, tokens(t)].bitcast(F32), ALU.subtract).then_inc(s_low_ready, 1)

            def energy_low(t):
                dve.wait_ge(e_ready, t + 1)
                nc.vector.scalar_tensor_tensor(e_low[t % 2], psum[:, 7, :], SCALE_A, e_high[t % 2].bitcast(F32), ALU.mult, ALU.subtract).then_inc(e_low_ready, 1)

            def mean_of_s():
                dve.wait_ge(s_ready, NG)
                nc.vector.tensor_reduce(mean_sum[:], mean_parts[:], AX.X, ALU.add).then_inc(mean_step, 1)
                dve.wait_ge(mean_step, 1)
                nc.vector.tensor_scalar(mean_sum[:], mean_sum[:], 1.0 / N, None, ALU.mult).then_inc(mean_step, 1)
                dve.wait_ge(mean_step, 2)
                nc.vector.tensor_copy(mean_b[:], mean_sum[:].to_broadcast([P, P])).then_inc(mean_step, 1)

            def field_sums(t):
                dve.wait_ge(o_filled, t + 1)
                if t >= 1:
                    dve.wait_ge(ot_filled, t)
                nc.vector.tensor_copy(oT, psum[:, 6 if t < NG - 1 else 3, :]).then_inc(oT_ready, 1)

            def field(t, by_tokens):
                dve.wait_ge(exp_done, 2 * GB * (t + 1))
                nc.vector.tensor_reduce(rsum[:, group(t)], rsum2[:, group(t), :], AX.X, ALU.add).then_inc(rden_ready, 1)
                dve.wait_ge(rden_ready, 2 * t + 1)
                nc.vector.reciprocal(rden[:, group(t)], rsum[:, group(t)]).then_inc(rden_ready, 1)
                dve.wait_ge(rden_ready, 2 * t + 2)
                dve.wait_ge(sg_ready, NG)
                if t >= 1:
                    dve.wait_ge(x1_ready, t)
                for u in range(GB):
                    b = GB * t + u
                    last = nc.vector.scalar_tensor_tensor(z[:, u * P:(u + 1) * P], by_tokens[:, u * P:(u + 1) * P], rden[:, b:b + 1],
                                                          sg[:, b, :], ALU.mult, ALU.add)
                    if t < NG - 1 or u < GB - 1:
                        last.then_inc(z_ready, 1)
                return last

            def norm1(t):
                dve.wait_ge(x1_ready, t + 1)
                for b in range(GB * t, GB * t + GB):
                    nc.vector.bn_stats(stats1[:, b, :], X1[:, b, :]).then_inc(y_stats, 1)
                for b in range(GB * t, GB * t + GB):
                    dve.wait_ge(y_stats, b + 1)
                    nc.vector.bn_aggr(mom1[:, b, :], stats1[:, b, :]).then_inc(y_mom, 1)

            def norm1_out(t):
                dve.wait_ge(y_pool, 5 * t + 2)
                dve.wait_ge(y_mom, GB * (t + 1))
                for b in range(GB * t, GB * t + GB):
                    nc.vector.tensor_scalar(Y[:, b, :], X1[:, b, :], mom1[:, b, 0:1], rs1[:, b:b + 1], ALU.subtract, ALU.mult).then_inc(y_ready, 1)

            energy_low(0)
            for n in range(NB):
                t, u = n // GB, n % GB
                for half in range(2):
                    dve.wait_ge(sc_filled, 2 * n + half + 1)
                    nc.vector.tensor_reduce(hmax[:, n, half:half + 1], psum[:, 2 * half:2 * half + 2, :], AX.XY, ALU.max).then_inc(max_found, 1)
                dve.wait_ge(max_found, 2 * n + 2)
                nc.vector.tensor_scalar(nbias[:, n:n + 1], hmax[:, n, 0:1], hmax[:, n, 1:2], -1.0, ALU.max, ALU.mult).then_inc(bias_ready, 1)
                if n == 0:
                    mean_of_s()
                if u == 1 and t < NG - 1:
                    energy_low(t + 1)
                if n == 1:
                    dve.wait_ge(gi_filled, 1)
                    nc.vector.tensor_copy(gi[:], psum[:, 6, 0:P]).then_inc(gi_ready, 1)
                if t >= 1 and u == 3:
                    field_sums(t - 1)
                if t >= 2 and u == 0:
                    dve.wait_ge(ot_filled, t - 1)
                    field(t - 2, psum[:, 6, :])
                if t >= 2 and u == 1:
                    norm1(t - 2)
                    norm1_out(t - 2)
            nc.vector.memset(kT[2 * KD:2 * KD + 1, 0, BANK:3 * BANK].bitcast(F32), 1.0).then_inc(k_one_set, 1)
            dve.wait_ge(ot_filled, NG - 1)
            field(NG - 2, psum[:, 6, :])

            route_steps = []

            def route_step(ins):
                ins.then_inc(route, 1)
                route_steps.append(ins)
                dve.wait_ge(route, len(route_steps))

            mask_marks = []
            for step in plan:
                kind, i = step[0], step[1] if len(step) > 1 else None
                T = turn.get(step)
                if kind == "lf" and i == NB - 1:
                    field_sums(NG - 1)
                elif kind == "lt":
                    dve.wait_ge(filled, T + 1)
                    field(NG - 1, misc(T)).then_inc(dve_emptied, 1)
                elif kind == "ln":
                    norm1(i)
                elif kind == "ly":
                    norm1_out(i)
                elif kind == "mx":
                    _, _, h, c = step
                    m = max_no[step]
                    k0, k1, diag = chunk(i, c)
                    dve.wait_ge(max_filled, m + 1)
                    if i >= 2:
                        dve.wait_ge(neg_max_ready, i - 1)
                    scores = psum[:, MX_BANKS[m % MB], :]
                    if diag > 0:
                        last = nc.vector.tensor_reduce(part_max[:, i % 2, h, c:c + 1], scores[:, 0:diag], AX.X, ALU.max)
                    if diag < k1 - k0:
                        if len(mask_marks) >= 2:
                            dve.wait_ge(max_emptied, mask_marks[-2])
                        spot = c + 1 if diag > 0 else c
                        last = nc.vector.tensor_tensor_reduce(out=masked[len(mask_marks) % 2][:], in0=scores[:, diag:k1 - k0], in1=fut[:], scale=1.0, scalar=-BIG,
                                                              op0=ALU.add, op1=ALU.max, accum_out=part_max[:, i % 2, h, spot:spot + 1])
                        mask_marks.append(m + 1)
                    last.then_inc(max_emptied, 1)
                elif kind == "nr":
                    spots = i // 4 + (2 if i % 4 else 1)
                    dve.wait_ge(max_emptied, max_no["mx", i, H - 1, i // 4] + 1)
                    if i >= 1:
                        dve.wait_ge(filled, turn["nm", i - 1] + 1)
                    nc.vector.tensor_reduce(neg_max[:, :], part_max[:, i % 2, :, 0:spots], AX.X, ALU.max, negate=True).then_inc(neg_max_ready, 1)
                elif kind == "yt":
                    src = misc(T)[:, :].rearrange("p (m g d) -> p m g d", m=HG, g=4)
                    dve.wait_ge(filled, T + 1)
                    if i >= 1:
                        dve.wait_ge(filled, turn["yn", i - 1] + 1)
                        wait_emptied(dve, turn["yt", i - 1])
                    nc.vector.reciprocal(yden, src[:, :, :, LAT]).then_inc(yden_ready, 1)
                    dve.wait_ge(yden_ready, i + 1)
                    nc.vector.tensor_tensor(ynorm.rearrange("p (g m) d -> p m g d", g=4), src[:, :, :, 0:LAT],
                                            yden.unsqueeze(3).to_broadcast([P, HG, 4, LAT]), ALU.mult).then_inc(dve_emptied, 1)
                elif kind == "yo":
                    dve.wait_ge(filled, T + 1)
                    nc.vector.tensor_tensor(hid[:, i, :], misc(T)[:, 0:P], Y[:, i, :], ALU.add).then_inc(dve_emptied, 1)
                    wait_emptied(dve, T)
                    nc.vector.bn_stats(stats2[:, i, :], hid[:, i, :]).then_inc(h_stats, 1)
                    dve.wait_ge(h_stats, i + 1)
                    nc.vector.bn_aggr(mom2[:, i, :], stats2[:, i, :]).then_inc(h_mom, 1)
                elif kind == "lg":
                    g, count = expert_blocks(i), EXPERT_BLOCKS[i][1]
                    dve.wait_ge(filled, T + 1)
                    nc.vector.tensor_tensor(logit[:, g, :], misc(T)[:, 0:count * E].rearrange("p (b e) -> p b e", b=count),
                                            ebias[:].unsqueeze(1).to_broadcast([P, count, E]), ALU.add).then_inc(dve_emptied, 1)
                    wait_emptied(dve, T)
                    route_step(nc.vector.tensor_reduce(lmax[:, g], logit[:, g, :], AX.X, ALU.max))
                    route_step(nc.vector.tensor_tensor(lshift[:, g, :], logit[:, g, :], lmax[:, g].unsqueeze(2).to_broadcast([P, count, E]), ALU.subtract))
                elif kind in ("ra", "rb", "rt"):
                    g, (first, count) = expert_blocks(i), EXPERT_BLOCKS[i]
                    iota_b = iot[:].unsqueeze(1).to_broadcast([P, count, E])
                if kind == "ra":
                    dve.wait_ge(lexp_ready, i + 1)
                    for b in range(first, first + count):
                        last = nc.vector.max(top[:, b, :], pe_[:, b, :])
                    route_step(last)
                    for b in range(first, first + count):
                        last = nc.vector.max_index(idx[:, b, :], top[:, b, :], pe_[:, b, :])
                    route_step(last)
                    route_step(nc.vector.tensor_copy(idxf[:, g, :], idx[:, g, 0:2]))
                elif kind == "rb":
                    route_step(nc.vector.tensor_tensor(pick0[:, g, :], iota_b, idxf[:, g, 0:1].to_broadcast([P, count, E]), ALU.is_equal))
                    route_step(nc.vector.tensor_tensor(pick1[:, g, :], iota_b, idxf[:, g, 1:2].to_broadcast([P, count, E]), ALU.is_equal))
                    route_step(nc.vector.tensor_tensor(pick[:, g, :], pick0[:, g, :], pick1[:, g, :], ALU.add))
                elif kind == "rt":
                    route_step(nc.vector.tensor_tensor(chosen[:, g, :], pick[:, g, :], pe_[:, g, :], ALU.mult))
                    route_step(nc.vector.tensor_reduce(csum[:, g], chosen[:, g, :], AX.X, ALU.add))
                    route_step(nc.vector.reciprocal(crec[:, g], csum[:, g]))
                    route_step(nc.vector.tensor_tensor(comb[:, g, :], chosen[:, g, :], crec[:, g].unsqueeze(2).to_broadcast([P, count, E]), ALU.mult))
                    assert len(route_steps) == ROUTE_STEPS * (i + 1)
                elif kind == "eu":
                    k, width = step[2], EXPERT_BLOCKS[i][1] * P
                    rows = P if k < 4 else EI
                    wait_emptied(dve, turn["eg", i, k])
                    if 5 * i + k >= 1:
                        wait_emptied(dve, turn["eu", (5 * i + k - 1) // 5, (5 * i + k - 1) % 5])
                    nc.vector.scalar_tensor_tensor(ga[0:rows, 0:width], tg[0:rows, 0:width], 1.0, gs[0:rows, 0:width], ALU.add, ALU.mult).then_inc(ga_done, 1)
                    dve.wait_ge(ga_done, 5 * i + k + 1)
                    dve.wait_ge(filled, T + 1)
                    if i >= 1 and k == 0:
                        dve.wait_ge(filled, turn["ed", i - 1] + 1)
                    nc.vector.tensor_tensor(hT[0:rows, k, 0:width], ga[0:rows, 0:width], misc(T)[0:rows, 0:width], ALU.mult).then_inc(dve_emptied, 1)
                elif kind == "ec":
                    k, width = step[2], EXPERT_BLOCKS[i][1] * P
                    wait_emptied(dve, turn["eu", i, k])
                    dve.wait_ge(filled, T + 1)
                    nc.vector.tensor_tensor(hT[:, k, 0:width], hT[:, k, 0:width], misc(T)[:, 0:width], ALU.mult).then_inc(dve_emptied, 1)
                elif kind == "ed":
                    count = EXPERT_BLOCKS[i][1]
                    dve.wait_ge(filled, T + 1)
                    dve.wait_ge(x1h_ready, i + 1)
                    if i >= 1:
                        dve.wait_ge(out_done[i - 1], 16)
                    nc.vector.tensor_tensor(res[:, 0:count * P].rearrange("p (b c) -> p b c", b=count),
                                            misc(T)[:, 0:count * P].rearrange("p (b c) -> p b c", b=count),
                                            x1h[:, expert_blocks(i), :], ALU.add).then_inc(dve_emptied, 1)

        @block.gpsimd
        def _(pool):
            nc.gpsimd.memset(half_neg[:], -0.5).then_inc(const_set, 1)
            nc.gpsimd.memset(val[:], 0.0).then_inc(const_set, 1)
            pool.wait_ge(const_set, 2)
            nc.gpsimd.memset(val[:, :, LAT:LAT + 1], 1.0).then_inc(const_set, 1)
            nc.gpsimd.memset(kv_diag[:], 0.0).then_inc(kv_zero, 1)
            for t in range(NG):
                g = group(t)
                pool.wait_ge(x_mom, GB * (t + 1))
                nc.gpsimd.tensor_scalar(var_e[:, g], mom[:, g, 1], EPS, None, ALU.add).then_inc(x_var, 1)
                pool.wait_ge(x_var, t + 1)
                nc.gpsimd.tensor_tensor(rstd[:, g], var_e[:, g], half_neg[:, g], ALU.pow).then_inc(x_rstd, 1)
            pool.wait_ge(gi_ready, 1)
            for t in range(NG):
                nc.gpsimd.tensor_tensor(sg[:, group(t), :], s_tok[:, group(t), :], gi[:].unsqueeze(1).to_broadcast([P, GB, P]), ALU.add).then_inc(sg_ready, 1)
            def residual1(t):
                g = group(t)
                pool.wait_ge(th_ready, t + 1)
                nc.gpsimd.tensor_tensor(X1[:, g, :], X[:, g, :], th[:].rearrange("p (b c) -> p b c", b=GB), ALU.add).then_inc(x1_ready, 1)

            def norm1(t):
                g = group(t)
                pool.wait_ge(y_mom, GB * (t + 1))
                nc.gpsimd.tensor_scalar(ve1[:, g], mom1[:, g, 1], EPS, None, ALU.add).then_inc(y_pool, 1)
                pool.wait_ge(y_pool, 5 * t + 1)
                nc.gpsimd.tensor_tensor(rs1[:, g], ve1[:, g], half_neg[:, 0:GB], ALU.pow).then_inc(y_pool, 1)
                pool.wait_ge(y_pool, 5 * t + 2)
                nc.gpsimd.tensor_tensor(sq1[:, g], rs1[:, g], rs1[:, g], ALU.mult).then_inc(y_pool, 1)
                pool.wait_ge(y_pool, 5 * t + 3)
                nc.gpsimd.tensor_tensor(ms1[:, g], sq1[:, g], mom1[:, g, 1], ALU.mult).then_inc(y_pool, 1)
                pool.wait_ge(y_pool, 5 * t + 4)
                nc.gpsimd.tensor_scalar(me1[:, g], ms1[:, g], EPS, None, ALU.add).then_inc(y_pool, 1)
                pool.wait_ge(y_pool, 5 * t + 5)
                nc.gpsimd.tensor_tensor(rr1[:, g], me1[:, g], half_neg[:, 0:GB], ALU.pow).then_inc(y_rms, 1)
                pool.wait_ge(y_rms, t + 1)
                pool.wait_ge(y_ready, GB * (t + 1))
                for b in range(GB * t, GB * t + GB):
                    nc.gpsimd.tensor_scalar(YR[:, b, :], Y[:, b, :], rr1[:, b:b + 1], None, ALU.mult).then_inc(yr_ready, 1)

            def follow(step):
                kind, i = step[0], step[1] if len(step) > 1 else None
                if kind == "lh":
                    residual1(NG - 1)
                elif kind == "ln":
                    norm1(i)
                elif kind == "qp":
                    mid = LAT + ROPE // 2
                    h0, h1 = HALVES[step[2]]
                    done = 2 * i + step[2]
                    part, turned = raw[:, h0:h1, :], rot[:, h0:h1, :]
                    high, low = qs[:, h0:h1, 0, :], qs[:, h0:h1, 1, :]
                    table = lambda values: values.to_broadcast([P, h1 - h0, values.shape[2]])
                    wait_emptied(pool, turn[step])
                    if i >= 1:
                        pool.wait_ge(filled, turn["tq", i - 1, 2 * step[2] + 1] + 1)
                    nc.gpsimd.tensor_tensor(turned[:, :, 0:ROPE // 2], part[:, :, mid:KD], table(sn[:, i:i + 1, 0:ROPE // 2]), ALU.mult).then_inc(rotated, 1)
                    nc.gpsimd.tensor_tensor(turned[:, :, ROPE // 2:ROPE], part[:, :, LAT:mid], table(sn[:, i:i + 1, ROPE // 2:ROPE]), ALU.mult).then_inc(rotated, 1)
                    pool.wait_ge(rotated, 4 * done + 2)
                    nc.gpsimd.tensor_tensor(part[:, :, LAT:KD], part[:, :, LAT:KD], table(cs[:, i:i + 1, :]), ALU.mult).then_inc(rotated, 1)
                    pool.wait_ge(rotated, 4 * done + 3)
                    nc.gpsimd.tensor_tensor(part[:, :, LAT:KD], part[:, :, LAT:KD], turned, ALU.add).then_inc(rotated, 1)
                    pool.wait_ge(rotated, 4 * done + 4)
                    nc.gpsimd.tensor_scalar(high, part, 1.0, None, ALU.mult).then_inc(q_high, 1)
                    pool.wait_ge(q_high, 2 * done + 1)
                    if h0 == 0:
                        nc.gpsimd.tensor_copy(val[:, i, 0:LAT], part[:, 0, 0:LAT])
                    nc.gpsimd.tensor_tensor(low, part, high.bitcast(F32), ALU.subtract).then_inc(q_high, 1)
                    pool.wait_ge(q_high, 2 * done + 2)
                    if h0 == 0:
                        nc.gpsimd.tensor_scalar(ks[:, :, 0, :], qs[:, 0, :, :].bitcast(F32), 1.0, None, ALU.mult)
                        nc.gpsimd.tensor_scalar(ks[:, :, 1, :], qs[:, 0, :, :].bitcast(F32), 1.0, None, ALU.mult).then_inc(q_split, 1)
                elif kind == "st" and step[3] == i:
                    g = step[2]
                    n = tile_no[i, g, i]
                    pool.wait_ge(tile_exp, n + 1)
                    tile = pb[:, n % SLOTS, :].rearrange("p (h q) -> p h q", h=HG)
                    nc.gpsimd.affine_select(out=tile, in_=tile, compare_op=ALU.is_ge, fill=0.0, base=0,
                                            pattern=[[0, HG], [1, P]], channel_multiplier=-1).then_inc(tile_masked, 1)
                elif kind == "yo" and i + 1 in [first + count for first, count in EXPERT_BLOCKS]:
                    t = [first + count for first, count in EXPERT_BLOCKS].index(i + 1)
                    g = expert_blocks(t)
                    pool.wait_ge(h_mom, i + 1)
                    nc.gpsimd.tensor_tensor(ms2[:, g], mom2[:, g, 0], mom2[:, g, 0], ALU.mult).then_inc(h_pool, 1)
                    pool.wait_ge(h_pool, 4 * t + 1)
                    nc.gpsimd.tensor_tensor(ms2[:, g], ms2[:, g], mom2[:, g, 1], ALU.add).then_inc(h_pool, 1)
                    pool.wait_ge(h_pool, 4 * t + 2)
                    nc.gpsimd.tensor_scalar(ms2[:, g], ms2[:, g], EPS, None, ALU.add).then_inc(h_pool, 1)
                    pool.wait_ge(h_pool, 4 * t + 3)
                    nc.gpsimd.tensor_tensor(r2[:, g], ms2[:, g], half_neg[:, g], ALU.pow).then_inc(h_pool, 1)
                    pool.wait_ge(h_pool, 4 * t + 4)
                    for b in range(EXPERT_BLOCKS[t][0], i + 1):
                        nc.gpsimd.tensor_scalar(xn2[:, b, :], hid[:, b, :], r2[:, b:b + 1], None, ALU.mult).then_inc(xn2_ready, 1)
                    nc.gpsimd.tensor_tensor(x1h[:, g, :], X1[:, g, :], hid[:, g, :], ALU.add).then_inc(x1h_ready, 1)
                elif kind == "rt":
                    g, count = expert_blocks(i), EXPERT_BLOCKS[i][1]
                    pool.wait_ge(route, ROUTE_STEPS * (i + 1))
                    if i >= 1:
                        pool.wait_ge(filled, turn["ec", i - 1, 3] + 1)
                    wide = comb_b[:, 0:count, :].rearrange("p b (e n) -> p (b e) n", e=E)
                    narrow = comb[:, g, :].rearrange("p b e -> p (b e)").unsqueeze(2).to_broadcast([P, count * E, EI])
                    nc.gpsimd.tensor_copy(wide, narrow).then_inc(comb_ready, 1)

            for n in range(2 * GB, NB):
                if n % GB == 1:
                    residual1(n // GB - 2)
                    norm1(n // GB - 2)
                for m in range(EARLY):
                    if (n, m) in early:
                        follow(early[n, m])
            residual1(NG - 2)
            for step in plan:
                follow(step)


_OUT = [((1, 2048, 128), "float32")]


def kernel(**inputs):
    import numpy as _np
    import concourse.bacc as _bacc
    from concourse import mybir as _mybir
    from concourse.bass_utils import run_bass_kernel_spmd as _run

    a = {k: _np.asarray(v) for k, v in inputs.items()}
    wq = a["L0_ffn_Wq"].reshape(P, H, 64)
    wkva = a["L0_ffn_Wkva"]
    pairs_first = _np.concatenate([_np.arange(0, ROPE, 2), _np.arange(1, ROPE, 2)])
    w_all = _np.zeros((P, H + 1, KD), _np.float32)
    w_all[:, 1:, LAT:] = wq[:, :, NOPE + pairs_first]
    w_all[:, 0, :LAT] = wkva[:, :LAT]
    w_all[:, 0, LAT:] = wkva[:, LAT + pairs_first]
    by_quarter = lambda w: w.reshape(4, P, -1).transpose(1, 0, 2)
    w_nope = by_quarter(wq[:, :, :NOPE].transpose(1, 2, 0).reshape(H * NOPE, P))
    w_kv = by_quarter(a["L0_ffn_Wkvb"].T)
    w_out = by_quarter(a["L0_ffn_Wo"].reshape(H, 64, P)[:, :NOPE].reshape(H * NOPE, P))
    with_shared = lambda w, s: _np.concatenate([w, s]).transpose(1, 0, 2)
    freqs = (_np.float32(1.0) / _np.float32(100000.0) ** (_np.arange(0, ROPE, 2, dtype=_np.float32) / _np.float32(ROPE))).astype(_np.float32)
    ang = _np.outer(_np.arange(N, dtype=_np.float32), freqs).astype(_np.float32)
    c, s = _np.cos(ang), _np.sin(ang)
    by_block = lambda t: t.reshape(NB, P, ROPE).transpose(1, 0, 2)
    cos = by_block(_np.concatenate([c, c], 1))
    sin = by_block(_np.concatenate([-s, s], 1))
    column = lambda v: v.reshape(P, 1)
    arrays = {
        "x": a["L0_attn_x"].reshape(N, P),
        "w_spin": a["L0_attn_W_spin"].T, "b_spin": column(a["L0_attn_b_spin"]), "w_global": a["L0_attn_W_global"].T,
        "w_j": a["L0_attn_W_J"].T, "beta": _np.broadcast_to(a["L0_attn_beta"], (P, 1)),
        "w_ln1": column(a["L0_ffn_w_ln1"]), "w_ln2": column(a["L0_ffn_w_ln2"]),
        "w_nope": w_nope, "w_all": w_all, "w_kv": w_kv, "w_out": w_out,
        "w_gate": a["L0_ffn_Wgate"], "e_bias": _np.broadcast_to(a["L0_ffn_expert_bias"], (P, E)),
        "w_eg": with_shared(a["L0_ffn_Wg"], a["L0_ffn_sWg"]), "w_eu": with_shared(a["L0_ffn_Wu"], a["L0_ffn_sWu"]),
        "w_ed": a["L0_ffn_Wd"].reshape(E // 2, P, P).transpose(1, 0, 2), "w_sd": a["L0_ffn_sWd"].reshape(EI, P),
        "ident": _np.eye(P, dtype=_np.float32), "future": _np.triu(_np.full((P, P), -BIG, _np.float32), 1),
        "iota": _np.broadcast_to(_np.arange(E, dtype=_np.float32), (P, E)), "cos": cos, "sin": sin,
    }
    nc = _bacc.Bacc("TRN2", target_bir_lowering=False, num_devices=1)
    maps, args = {}, []
    for name, v in arrays.items():
        v = _np.ascontiguousarray(v)
        maps[f"in_{name}"] = v
        args.append(nc.dram_tensor(f"in_{name}", v.shape, _mybir.dt.from_np(v.dtype), kind="ExternalInput").ap())
    args.append(nc.dram_tensor("out_0", (N, P), _mybir.dt.float32, kind="ExternalOutput").ap())
    build(nc, *args)
    r = _run(nc, [maps], core_ids=[0])
    return r.results[0]["out_0"].reshape(_OUT[0][0])
```
